# Optimizing a Trainium2 kernel written in Bass

```python
import numpy as np
import jax
import jax.numpy as jnp

def _softmax(x, axis=-1):
    return jax.nn.softmax(x, axis=axis)

def _gelu(x):
    return jax.nn.gelu(x, approximate=True)

def _silu(x):
    return jax.nn.silu(x)

def _sigmoid(x):
    return jax.nn.sigmoid(x)

def _layernorm(x, axis=-1, eps=1e-05):
    m = jnp.mean(x, axis=axis, keepdims=True)
    v = jnp.var(x, axis=axis, keepdims=True)
    return (x - m) / jnp.sqrt(v + eps)

def _scatter_add(tgt, idx, src, axis=0):
    return tgt.at[idx].add(src)

def _segment_sum(src, seg, n):
    return jax.ops.segment_sum(src, seg, n)
kernel_name = 'mk_seq_postln_d1_jaxref_r4_4009cc'

def setup_inputs(seed: int=0):
    np.random.seed(seed)
    _w = jnp.asarray

    def _L0_attn_setup():
        import jax, jax.numpy as jnp
        import numpy as np
        D_MODEL = 256
        NHEAD = 16
        HEAD_DIM = D_MODEL // NHEAD
        B, L = (4, 1024)
        LN_EPS = 1e-05

        def _retention(v, lam):

            def step(state, v_t):
                state = lam[None, :, None] * state + v_t
                return (state, state)
            v_l_first = jnp.swapaxes(v, 0, 1)
            init = jnp.zeros(v_l_first.shape[1:], dtype=v.dtype)
            _, states = jax.lax.scan(step, init, v_l_first)
            return jnp.swapaxes(states, 0, 1)
        key = jax.random.key(seed)
        ks = jax.random.split(key, 8)
        x = jax.random.normal(ks[0], (B, L, D_MODEL), dtype=jnp.float32)
        sin = jnp.zeros((L, HEAD_DIM), dtype=jnp.float32)
        cos = jnp.zeros((L, HEAD_DIM), dtype=jnp.float32)
        decay = jax.random.uniform(ks[1], (NHEAD, 2, 1), dtype=jnp.float32)
        scale = 0.02
        Wq = jax.random.normal(ks[2], (D_MODEL, D_MODEL), dtype=jnp.float32) * scale
        Wv = jax.random.normal(ks[3], (D_MODEL, D_MODEL), dtype=jnp.float32) * scale
        Wo = jax.random.normal(ks[4], (D_MODEL, D_MODEL), dtype=jnp.float32) * scale
        Wg = jax.random.normal(ks[5], (D_MODEL, D_MODEL), dtype=jnp.float32) * scale
        ln_g = jnp.ones((D_MODEL,), dtype=jnp.float32)
        ln_b = jnp.zeros((D_MODEL,), dtype=jnp.float32)
        return {'x': x, 'sin': sin, 'cos': cos, 'decay': decay, 'Wq': Wq, 'Wv': Wv, 'Wo': Wo, 'Wg': Wg, 'ln_g': ln_g, 'ln_b': ln_b}
    _L0_attn_in = _L0_attn_setup()

    def _L0_ffn_setup():
        import jax, jax.numpy as jnp
        import numpy as np
        TOP_K = 2
        N_EXPERTS = 8
        key = jax.random.key(seed)
        k_x, k_g, k_w1, k_w2 = jax.random.split(key, 4)
        B, S, d_in, d_hid, d_out, E = (8, 512, 256, 512, 256, N_EXPERTS)
        s_gate = float(np.sqrt(6.0 / (d_in + E)))
        s_w1 = float(np.sqrt(6.0 / (d_in + d_hid)))
        s_w2 = float(np.sqrt(6.0 / (d_hid + d_out)))
        x = jax.random.normal(k_x, (B, S, d_in), dtype=jnp.float32)
        gate_W = jax.random.uniform(k_g, (d_in, E), jnp.float32, -s_gate, s_gate)
        W1 = jax.random.uniform(k_w1, (E, d_in, d_hid), jnp.float32, -s_w1, s_w1)
        b1 = jnp.zeros((E, d_hid), jnp.float32)
        W2 = jax.random.uniform(k_w2, (E, d_hid, d_out), jnp.float32, -s_w2, s_w2)
        b2 = jnp.zeros((E, d_out), jnp.float32)
        return {'x': x, 'gate_W': gate_W, 'W1': W1, 'b1': b1, 'W2': W2, 'b2': b2}
    _L0_ffn_in = _L0_ffn_setup()
    _d = {'L0_attn_x': _L0_attn_in['x'], 'L0_attn_sin': _L0_attn_in['sin'], 'L0_attn_cos': _L0_attn_in['cos'], 'L0_attn_decay': _L0_attn_in['decay'], 'L0_attn_Wq': _L0_attn_in['Wq'], 'L0_attn_Wv': _L0_attn_in['Wv'], 'L0_attn_Wo': _L0_attn_in['Wo'], 'L0_attn_Wg': _L0_attn_in['Wg'], 'L0_attn_ln_g': _L0_attn_in['ln_g'], 'L0_attn_ln_b': _L0_attn_in['ln_b'], 'L0_ffn_gate_W': _L0_ffn_in['gate_W'], 'L0_ffn_W1': _L0_ffn_in['W1'], 'L0_ffn_b1': _L0_ffn_in['b1'], 'L0_ffn_W2': _L0_ffn_in['W2'], 'L0_ffn_b2': _L0_ffn_in['b2']}
    _x0 = _d['L0_attn_x']
    _d['L0_attn_x'] = jax.random.normal(jax.random.fold_in(jax.random.key(seed), 1), (2, 4096, 256), dtype=_x0.dtype)
    del _x0
    return _d

def reference(L0_attn_x, L0_attn_sin, L0_attn_cos, L0_attn_decay, L0_attn_Wq, L0_attn_Wv, L0_attn_Wo, L0_attn_Wg, L0_attn_ln_g, L0_attn_ln_b, L0_ffn_gate_W, L0_ffn_W1, L0_ffn_b1, L0_ffn_W2, L0_ffn_b2):

    def _L0_attn_ref(x, sin, cos, decay, Wq, Wv, Wo, Wg, ln_g, ln_b):
        import jax, jax.numpy as jnp
        import numpy as np
        D_MODEL = 256
        NHEAD = 16
        HEAD_DIM = D_MODEL // NHEAD
        B, L = (4, 1024)
        LN_EPS = 1e-05

        def _retention(v, lam):

            def step(state, v_t):
                state = lam[None, :, None] * state + v_t
                return (state, state)
            v_l_first = jnp.swapaxes(v, 0, 1)
            init = jnp.zeros(v_l_first.shape[1:], dtype=v.dtype)
            _, states = jax.lax.scan(step, init, v_l_first)
            return jnp.swapaxes(states, 0, 1)
        del sin, cos
        Bx, Lx, D = x.shape
        H = decay.shape[0]
        Dh = D // H
        q = (x @ Wq.T).reshape(Bx, Lx, H, Dh)
        v = (x @ Wv.T).reshape(Bx, Lx, H, Dh)
        lam = decay[:, 1, 0]
        state = _retention(v, lam)
        y = (q * state).reshape(Bx, Lx, D)
        mu = jnp.mean(y, axis=-1, keepdims=True)
        var = jnp.mean(jnp.square(y - mu), axis=-1, keepdims=True)
        y = (y - mu) * jax.lax.rsqrt(var + LN_EPS) * ln_g + ln_b
        gate = jax.nn.silu(x @ Wg.T)
        y = y * gate
        return y @ Wo.T

    def _L0_ffn_ref(x, gate_W, W1, b1, W2, b2):
        import jax, jax.numpy as jnp
        import numpy as np
        TOP_K = 2
        N_EXPERTS = 8
        E = W1.shape[0]
        d_in = x.shape[-1]
        d_out = W2.shape[-1]
        x_flat = x.reshape(-1, d_in)
        logits = x_flat @ gate_W
        gates = jax.nn.softmax(logits, axis=-1)
        tk_g, tk_i = jax.lax.top_k(gates, TOP_K)
        tk_g = tk_g / (jnp.sum(tk_g, axis=-1, keepdims=True) + 1e-08)
        cw = jnp.sum(jax.nn.one_hot(tk_i, E, dtype=x.dtype) * tk_g[..., None], axis=1)
        out = x_flat
        for e in range(E):
            h = jax.nn.relu(x_flat @ W1[e] + b1[e])
            out = out + cw[:, e:e + 1] * (h @ W2[e] + b2[e])
        return out.reshape(x.shape[:-1] + (d_out,))
    x = L0_attn_x
    x = _layernorm(x + _L0_attn_ref(x, L0_attn_sin, L0_attn_cos, L0_attn_decay, L0_attn_Wq, L0_attn_Wv, L0_attn_Wo, L0_attn_Wg, L0_attn_ln_g, L0_attn_ln_b), axis=-1)
    x = _layernorm(x + _L0_ffn_ref(x, L0_ffn_gate_W, L0_ffn_W1, L0_ffn_b1, L0_ffn_W2, L0_ffn_b2), axis=-1)
    return x

_drawn_inputs = setup_inputs


def setup_inputs(seed=0):
    import zlib

    import numpy as np

    out = dict(_drawn_inputs(seed))
    spreads = {'L0_attn_sin': (0.0, 0.1),
     'L0_attn_cos': (0.0, 0.1),
     'L0_attn_ln_g': (1.0, 0.6),
     'L0_attn_ln_b': (0.0, 0.57),
     'L0_ffn_b1': (0.0, 0.268),
     'L0_ffn_b2': (0.0, 0.1)}
    factors = {}
    for name, (base, spread) in spreads.items():
        noise = np.random.default_rng([zlib.crc32(name.encode()), seed]).standard_normal(out[name].shape)
        drawn = base * np.exp(spread * noise) if base else spread * noise
        out[name] = jnp.asarray(drawn.astype(out[name].dtype))
    for name, factor in factors.items():
        out[name] = (out[name] * factor).astype(out[name].dtype)
    return out
```

```python
from contextlib import ExitStack

import concourse.bass as bass
from concourse import mybir

F32 = mybir.dt.float32
F16 = mybir.dt.float16
U32 = mybir.dt.uint32
I32 = mybir.dt.int32
ALU = mybir.AluOpType
ACT = mybir.ActivationFunctionType
AX_X = mybir.AxisListType.X

P = 128
D = 256
DC = D // P
E = 8
HID = 512
HC = HID // P
TOKENS = 8192
BLK = 512
NB = TOKENS // BLK
BLOCKS_PER_SEQ = 8
S = BLK // P
TILE = 256
TS = TILE // P
REGION = TOKENS + TILE
TILES = (2 * TOKENS + E * (TILE - 1)) // TILE
ROW = 528
ROWF = ROW // 2
META = 2 * D // 2
NO_TOKEN = 20000.0
WSCALE = 64.0
LN_EPS = 1e-05
W_Q, W_V, W_G, W_O = range(4)


def wait(eng, sem, value, beside=None):
    if not isinstance(value, int) or value > 0:
        if beside is not None and not isinstance(value, int):
            eng.wait_ge(*beside)
        eng.wait_ge(sem, value)


def build_attend(nc, io, keep):
    x1, wf16, m8, count_acc = keep["x1"], keep["wf16"], keep["m8"], keep["count_acc"]
    region = io["region"]
    with ExitStack() as ctx:
        def sb(name, shape, dt):
            return ctx.enter_context(nc.sbuf_tensor(name, shape, dt))

        def sem(name):
            return ctx.enter_context(nc.semaphore(name))

        ident = sb("ident", [P, P], F32)
        tri_ones = keep["tri_ones"]
        iota_e = sb("iota_e", [P, E], F32)
        region_base = sb("region_base", [P, E], F32)
        token0 = sb("token0", [P, S], F32)
        keep_state = sb("keep_state", [P, NB + 1], F32)
        half_pow = sb("half_pow", [P, S], F32)
        eps = sb("eps", [P, S], F32)
        minus_one = sb("minus_one", [P, S], F32)
        blk = sb("blk", [P, S], F32)
        lam = sb("lam", [P, DC], F32)
        ln_gb = sb("ln_gb", [P, 2, DC], F32)
        gate_w = sb("gate_w", [P, DC, E], F32)
        wa_hi = sb("wa_hi", [P, 4, DC, D], F16)
        wa_lo = sb("wa_lo", [P, 4, DC, D], F16)
        xT32 = [sb(f"xT32_{u}", [P, DC * BLK], F32) for u in range(2)]
        xT_hi = sb("xT_hi", [P, DC, BLK], F16)
        xT_lo = sb("xT_lo", [P, DC, BLK], F16)
        x_tok = [sb(f"x_tok_{u}", [P, S * D], F32) for u in range(2)]
        carry = sb("carry", [P, DC], F32)
        y = sb("y", [P, DC, BLK], F32)
        gate = [sb(f"gate_{u}", [P, DC * BLK], F32) for u in range(2)]
        wa32 = gate[1][:, :].rearrange("p (w d) -> p w d", w=4)
        yn = sb("yn", [P, DC * BLK], F32)
        z_hi = sb("z_hi", [P, DC, BLK], F16)
        z_lo = sb("z_lo", [P, DC, BLK], F16)
        row = [sb(f"row_{u}", [P, S, ROWF], F32) for u in range(2)]
        x1_new = [sb(f"x1_new_{u}", [P, S * D], F32) for u in range(2)]
        x1T = sb("x1T", [P, DC * BLK], F32)
        wf32 = sb("wf32", [P, DC * HID], F32)
        bn_y = sb("bn_y", [P, S, 6], F32)
        mv_y = sb("mv_y", [P, S, 2], F32)
        rs_y = sb("rs_y", [P, 3, S], F32)
        bn_x = sb("bn_x", [P, S, 6], F32)
        mv_x = sb("mv_x", [P, S, 2], F32)
        rs_x = sb("rs_x", [P, 3, S], F32)
        logits = sb("logits", [P, S, E], F32)
        m8_new = sb("m8_new", [P, S, E], F32)
        i8 = sb("i8", [P, S, E], U32)
        chosen = sb("chosen", [P, 2, S], F32)
        onehot = sb("onehot", [P, 2, S, E], F32)
        mask = sb("mask", [P, S, E], F16)
        block_sum = sb("block_sum", [P, E], F32)
        position = sb("position", [P, S, E], F32)
        picked = sb("picked", [P, 2, S, E], F32)
        slot = [sb(f"slot_{u}", [P, 2, S], U32) for u in range(2)]
        token = sb("token", [P, S], F32)

        ps_a = ctx.enter_context(nc.psum_tensor("ps_a", [P, 3 * BLK], F32))
        ps_b = ctx.enter_context(nc.psum_tensor("ps_b", [P, 3 * BLK], F32))
        ps_t = ctx.enter_context(nc.psum_tensor("ps_t", [P, 2 * BLK], F32))
        vqg = [ps_a, ps_b]
        yT = ps_a[:, 0:2 * BLK]
        ps_logits = ps_a[:, 2 * BLK:2 * BLK + S * E]
        ps_pos = ps_a[:, 2 * BLK + 64:2 * BLK + 64 + S * E]

        par_in = sem("par_in")
        wa_in = [sem("wa_in_0"), sem("wa_in_1")]
        xT_in = [sem("xT_in_0"), sem("xT_in_1")]
        xtok_in = [sem("xtok_in_0"), sem("xtok_in_1")]
        wf_in = sem("wf_in")
        x1_kept = [sem("x1_kept_0"), sem("x1_kept_1")]
        scattered = [sem("scattered_0"), sem("scattered_1")]
        set_done = sem("set_done")
        wa_hi_done = sem("wa_hi_done")
        wa_lo_done = sem("wa_lo_done")
        x_hi = sem("x_hi")
        x_lo = sem("x_lo")
        projected = sem("projected")
        tanh_done = sem("tanh_done")
        scanned = sem("scanned")
        gated = sem("gated")
        y_done = sem("y_done")
        carried = sem("carried")
        y_by_token = sem("y_by_token")
        bn_y_done = sem("bn_y_done")
        stats_y = sem("stats_y")
        rstd_y_step = sem("rstd_y_step")
        rstd_y = sem("rstd_y")
        y_normed = sem("y_normed")
        yn_by_channel = sem("yn_by_channel")
        affine = sem("affine")
        z_done = sem("z_done")
        zhi_done = sem("zhi_done")
        zlo_done = sem("zlo_done")
        out_projected = sem("out_projected")
        residual = sem("residual")
        bn_x_done = sem("bn_x_done")
        stats_x = sem("stats_x")
        rstd_x_step = sem("rstd_x_step")
        rstd_x = sem("rstd_x")
        x1_done = sem("x1_done")
        row_hi = sem("row_hi")
        row_lo = sem("row_lo")
        x1_by_channel = sem("x1_by_channel")
        x1T_done = sem("x1T_done")
        routed = sem("routed")
        logits_read = sem("logits_read")
        top_done = sem("top_done")
        top_kept = sem("top_kept")
        index_done = sem("index_done")
        chosen_done = sem("chosen_done")
        onehot_done = sem("onehot_done")
        mask_done = sem("mask_done")
        summed = sem("summed")
        counted = sem("counted")
        pos_done = sem("pos_done")
        pos_read = sem("pos_read")
        picked_done = sem("picked_done")
        slots_done = sem("slots_done")
        meta_done = sem("meta_done")
        token_next = sem("token_next")
        wf_scaled = sem("wf_scaled")
        wf_hi_done = sem("wf_hi_done")
        wf_lo_done = sem("wf_lo_done")

        N_PAR = 9

        def pipeline(eng, step):
            for i in range(4):
                step(i // 2, i % 2, True, i >= 1, i >= 2)
            with eng.Fori(2, NB // 2 - 1) as j:
                for u in range(2):
                    step(j, u, True, True, True)
            for u in range(2):
                step(NB // 2 - 1, u, True, True, True)
            step(NB // 2, 0, False, True, True)
            step(NB // 2, 1, False, False, True)

        block = ctx.enter_context(nc.Block())

        @block.sync
        def _(sp):
            for dst, src in ((ident[:, :], io["ident"]), (tri_ones[:, :, :], io["tri_ones"]),
                             (iota_e[:, :], io["iota_e"]), (region_base[:, :], io["region_base"]),
                             (token0[:, :], io["token0"]), (keep_state[:, :], io["keep_state"]),
                             (lam[:, :], io["lam"]), (ln_gb[:, :, :], io["ln_gb"]),
                             (gate_w[:, :, :], io["gate_w"])):
                sp.dma_start(dst, src).then_inc(par_in, 16)

            def keep_x1(b, u):
                sp.dma_start(x1[:, bass.ds(b * S * D, S * D)], x1_new[u][:, :]).then_inc(x1_kept[u], 16)

            def load(j, u):
                i = 2 * j + u
                wait(sp, x_hi, i - 1)
                wait(sp, x_lo, i - 1)
                sp.dma_start(xT32[u][:, :], io["xT"][i]).then_inc(xT_in[u], 16)
                if isinstance(i, int) and i < 2:
                    wait(sp, wa_lo_done, i)
                    sp.dma_start(wa32[:, :, :], io["wa"][i]).then_inc(wa_in[u], 16)
                wait(sp, wf_hi_done, i)
                wait(sp, wf_lo_done, i)
                sp.dma_start(wf32[:, :], io["wf"][i]).then_inc(wf_in, 16)
                if not (isinstance(i, int) and i == 0):
                    load_tokens(i - 1, 1 - u)

            def load_tokens(b, u):
                wait(sp, x1_done, b - 1)
                sp.dma_start(x_tok[u][:, :].rearrange("p (s d) -> p s d", s=S),
                             io["x_tok"][b]).then_inc(xtok_in[u], 16)
                if not (isinstance(b, int) and b < 2):
                    keep_x1(b - 2, u)

            for i in range(4):
                load(i // 2, i % 2)
            with sp.Fori(2, NB // 2) as j:
                for u in range(2):
                    load(j, u)
            load_tokens(NB - 1, 1)
            for u in range(2):
                sp.wait_ge(x1_done, NB - 1 + u)
                keep_x1(NB - 2 + u, u)
            for u in range(2):
                sp.wait_ge(x1_kept[u], 16 * NB // 2)

        @block.tensor
        def _(pe):
            pe.wait_ge(par_in, 16 * N_PAR)
            pe.wait_ge(wa_lo_done, 2)
            pe.wait_ge(set_done, 1)

            def project(c):
                out = vqg[c]
                for n, w in enumerate((W_V, W_Q, W_G)):
                    dst = out[:, n * BLK:(n + 1) * BLK]
                    m = 0
                    for k in range(DC):
                        for a, b in ((wa_hi, xT_hi), (wa_lo, xT_hi), (wa_hi, xT_lo)):
                            last = nc.tensor.matmul(dst, a[:, w, k, c * P:(c + 1) * P], b[:, k, :],
                                                    start=(m == 0), stop=(m == 3 * DC - 1))
                            m += 1
                last.then_inc(projected, 1)

            def step(j, u, now, prev, prev2):
                i = 2 * j + u
                if now:
                    wait(pe, x_hi, i + 1)
                    wait(pe, x_lo, i + 1)
                    wait(pe, y_done, 2 * i - 1)
                    project(1)
                if prev:
                    wait(pe, y_normed, i)
                    wait(pe, residual, i - 1)
                    for c in range(DC):
                        for s in range(S):
                            last = nc.tensor.transpose(
                                ps_t[:, c * BLK + s * P:c * BLK + (s + 1) * P],
                                yn[:, s * D + c * P:s * D + (c + 1) * P], ident[:, :])
                    last.then_inc(yn_by_channel, 1)
                if now:
                    if prev2:
                        wait(pe, pos_read, i - 2)
                    project(0)
                if prev2:
                    wait(pe, x1_done, i - 1)
                    if prev:
                        wait(pe, affine, 2 * i)
                    for c in range(DC):
                        for s in range(S):
                            last = nc.tensor.transpose(
                                ps_t[:, c * BLK + s * P:c * BLK + (s + 1) * P],
                                x1_new[u][:, s * D + c * P:s * D + (c + 1) * P], ident[:, :])
                    last.then_inc(x1_by_channel, 1)
                if now:
                    wait(pe, y_done, 2 * i + 2)
                    for s in range(S):
                        for c in range(DC):
                            last = nc.tensor.transpose(yT[:, s * D + c * P:s * D + (c + 1) * P],
                                                       y[:, c, s * P:(s + 1) * P], ident[:, :])
                    last.then_inc(y_by_token, 1)
                if prev2:
                    wait(pe, x1T_done, i - 1)
                    if not now:
                        wait(pe, y_done, 2 * NB)
                        wait(pe, pos_read, i - 2)
                    for s in range(S):
                        for c in range(DC):
                            last = nc.tensor.matmul(ps_logits[:, s * E:(s + 1) * E],
                                                    x1T[:, c * BLK + s * P:c * BLK + (s + 1) * P],
                                                    gate_w[:, c, :], start=(c == 0), stop=(c == DC - 1))
                    last.then_inc(routed, 1)
                if prev:
                    wait(pe, zlo_done, i)
                    for s in range(S):
                        m = 0
                        for c in range(DC):
                            for a, b in ((z_hi, wa_hi), (z_lo, wa_hi), (z_hi, wa_lo)):
                                last = nc.tensor.matmul(ps_t[:, s * D:(s + 1) * D], a[:, c, s * P:(s + 1) * P],
                                                        b[:, W_O, c, :], start=(m == 0), stop=(m == 3 * DC - 1))
                                m += 1
                    last.then_inc(out_projected, 1)
                if prev2:
                    wait(pe, mask_done, i - 1)
                    wait(pe, counted, i - 2)
                    for s in range(S):
                        dst = ps_pos[:, s * E:(s + 1) * E]
                        nc.tensor.matmul(dst, tri_ones[:, 0, :], mask[:, s, :], start=True, stop=False)
                        for before in range(s):
                            nc.tensor.matmul(dst, tri_ones[:, 1, :], mask[:, before, :], start=False, stop=False)
                        last = nc.tensor.matmul(dst, tri_ones[:, 1, :], count_acc[:, :], start=False, stop=True)
                    last.then_inc(pos_done, 1)

            pipeline(pe, step)

        @block.vector
        def _(dve):
            v = nc.vector
            v.memset(carry[:, :], 0.0)
            v.memset(count_acc[:, :], 0.0)
            v.memset(half_pow[:, :], -0.5)
            v.memset(eps[:, :], LN_EPS)
            v.memset(minus_one[:, :], -1.0)
            v.memset(blk[:, :], float(BLK))
            for u in range(2):
                last = v.memset(row[u][:, :, :], 0.0)
            last.then_inc(set_done, 1)
            dve.wait_ge(par_in, 16 * N_PAR)
            dve.wait_ge(set_done, 1)
            v.tensor_scalar(ln_gb[:, :, :], ln_gb[:, :, :], 0.5 / WSCALE, None, ALU.mult).then_inc(set_done, 1)
            for h in range(2):
                dve.wait_ge(wa_hi_done, h + 1)
                v.scalar_tensor_tensor(out=wa_lo[:, :, h, :], in0=wa32[:, :, :], scalar=WSCALE,
                                       in1=wa_hi[:, :, h, :], op0=ALU.mult,
                                       op1=ALU.subtract).then_inc(wa_lo_done, 1)

            def retain(i, u, c):
                n = 1 - c
                wait(dve, projected, 2 * i + n + 1)
                wait(dve, carried, 2 * i + n - 1)
                if n == 0:
                    wait(dve, y_by_token, i)
                v.tensor_tensor_scan(y[:, c, :], lam[:, c:c + 1].broadcast_to([P, BLK]),
                                     vqg[c][:, 0:BLK], carry[:, c:c + 1], ALU.mult,
                                     ALU.add).then_inc(scanned, 1)
                wait(dve, tanh_done, 2 * i + n + 1)
                g = gate[u][:, c * BLK:(c + 1) * BLK]
                v.scalar_tensor_tensor(out=g, in0=g, scalar=1.0, in1=vqg[c][:, 2 * BLK:3 * BLK],
                                       op0=ALU.add, op1=ALU.mult).then_inc(gated, 1)
                wait(dve, scanned, 2 * i + n + 1)
                v.tensor_scalar(carry[:, c:c + 1], y[:, c, BLK - 1:BLK], keep_state[:, bass.ds(i + 1, 1)], None,
                                ALU.mult).then_inc(carried, 1)
                wait(dve, carried, 2 * i + n + 1)
                v.scalar_tensor_tensor(out=y[:, c, :], in0=vqg[c][:, BLK:2 * BLK],
                                       scalar=1.0 / (WSCALE * WSCALE), in1=y[:, c, :],
                                       op0=ALU.mult, op1=ALU.mult).then_inc(y_done, 1)

            def step(j, u, now, prev, prev2):
                i = 2 * j + u
                b = i - 2
                if now:
                    retain(i, u, 1)
                if prev:
                    wait(dve, affine, 2 * i)
                    wait(dve, gated, 2 * i)
                    v.tensor_tensor(yn[:, :], yn[:, :], gate[1 - u][:, :], ALU.mult).then_inc(z_done, 1)
                if now:
                    retain(i, u, 0)
                if prev:
                    wait(dve, zhi_done, i)
                    wait(dve, out_projected, i - 1)
                    v.tensor_tensor(z_lo[:, :, :], yn[:, :].rearrange("p (c t) -> p c t", c=DC),
                                    z_hi[:, :, :], ALU.subtract).then_inc(zlo_done, 1)
                if now:
                    wait(dve, y_by_token, i + 1)
                    for s in range(S):
                        last = v.bn_stats(bn_y[:, s, :], yT[:, s * D:(s + 1) * D])
                    last.then_inc(bn_y_done, 1)
                    wait(dve, bn_y_done, i + 1, beside=(set_done, 1))
                    wait(dve, rstd_y, i)
                    for s in range(S):
                        last = v.bn_aggr(mv_y[:, s, :], bn_y[:, s, :])
                    last.then_inc(stats_y, 1)
                if prev2:
                    wait(dve, row_hi, i - 1)
                    rowh = row[u][:, :, :].bitcast(F16)
                    v.tensor_tensor(rowh[:, :, D:2 * D],
                                    x1_new[u][:, :].rearrange("p (s d) -> p s d", s=S),
                                    rowh[:, :, 0:D], ALU.subtract).then_inc(row_lo, 1)
                if prev2:
                    wait(dve, routed, b + 1)
                    wait(dve, top_kept, b)
                    v.tensor_copy(logits[:, :, :], ps_logits.rearrange("p (s e) -> p s e", s=S)
                                  ).then_inc(logits_read, 1)
                    wait(dve, logits_read, b + 1, beside=(set_done, 1))
                    for s in range(S):
                        last = v.max(m8_new[:, s, :], logits[:, s, :])
                    last.then_inc(top_done, 1)
                    wait(dve, top_done, b + 1, beside=(set_done, 1))
                    for s in range(S):
                        last = v.max_index(i8[:, s, :], m8_new[:, s, :], logits[:, s, :])
                    last.then_inc(index_done, 1)
                    wait(dve, index_done, b + 1)
                    wait(dve, meta_done, 2 * b)
                    v.tensor_copy(chosen[:, :, :], i8[:, :, 0:2].rearrange("p s k -> p k s")
                                  ).then_inc(chosen_done, 1)
                    wait(dve, chosen_done, b + 1)
                    v.tensor_tensor(onehot[:, :, :, :],
                                    iota_e[:, :].unsqueeze(1).unsqueeze(1).broadcast_to([P, 2, S, E]),
                                    chosen[:, :, :].unsqueeze(3).broadcast_to([P, 2, S, E]),
                                    ALU.is_equal).then_inc(onehot_done, 1)
                    wait(dve, onehot_done, b + 1)
                    v.tensor_tensor(mask[:, :, :], onehot[:, 0, :, :], onehot[:, 1, :, :],
                                    ALU.add).then_inc(mask_done, 1)
                    wait(dve, mask_done, b + 1)
                    v.tensor_reduce(block_sum[:, :], mask[:, :, :].rearrange("p s e -> p e s"), AX_X,
                                    ALU.add).then_inc(summed, 1)
                if prev:
                    wait(dve, out_projected, i)
                    wait(dve, xtok_in[1 - u], 16 * (j + u))
                    t = x_tok[1 - u]
                    v.scalar_tensor_tensor(out=t[:, :], in0=ps_t[:, :], scalar=1.0 / WSCALE, in1=t[:, :],
                                           op0=ALU.mult, op1=ALU.add).then_inc(residual, 1)
                    wait(dve, residual, i)
                    for s in range(S):
                        last = v.bn_stats(bn_x[:, s, :], t[:, s * D:(s + 1) * D])
                    last.then_inc(bn_x_done, 1)
                    wait(dve, bn_x_done, i, beside=(set_done, 1))
                    wait(dve, rstd_x, i - 1)
                    for s in range(S):
                        last = v.bn_aggr(mv_x[:, s, :], bn_x[:, s, :])
                    last.then_inc(stats_x, 1)
                if prev2:
                    wait(dve, pos_done, b + 1)
                    v.tensor_tensor(position[:, :, :], ps_pos.rearrange("p (s e) -> p s e", s=S),
                                    region_base[:, :].unsqueeze(1).broadcast_to([P, S, E]),
                                    ALU.add).then_inc(pos_read, 1)
                    wait(dve, summed, b + 1)
                    v.tensor_tensor(count_acc[:, :], count_acc[:, :], block_sum[:, :], ALU.add).then_inc(counted, 1)
                    wait(dve, pos_read, b + 1)
                    v.tensor_tensor(picked[:, :, :, :], onehot[:, :, :, :],
                                    position[:, :, :].unsqueeze(1).broadcast_to([P, 2, S, E]),
                                    ALU.mult).then_inc(picked_done, 1)
                    wait(dve, picked_done, b + 1)
                    wait(dve, scattered[u], 128 * (j - 1))
                    with nc.allow_low_precision("row numbers are whole and below 2^24"):
                        v.tensor_reduce(slot[u][:, :, :], picked[:, :, :, :], AX_X, ALU.add).then_inc(slots_done, 1)

            pipeline(dve, step)

        @block.scalar
        def _(act):
            a = nc.scalar
            for h in range(2):
                act.wait_ge(wa_in[h], 16)
                a.activation(wa_hi[:, :, h, :], wa32[:, :, :], ACT.Copy, scale=WSCALE).then_inc(wa_hi_done, 1)

            def split_x(b, u, loads):
                wait(act, xT_in[u], 16 * loads)
                wait(act, projected, 2 * b)
                a.activation(xT_hi[:, :, :], xT32[u][:, :].rearrange("p (c t) -> p c t", c=DC),
                             ACT.Copy).then_inc(x_hi, 1)

            split_x(0, 0, 1)

            def step(j, u, now, prev, prev2):
                i = 2 * j + u
                if now:
                    wait(act, projected, 2 * i + 1)
                    wait(act, z_done, i - 1)
                    a.activation(gate[u][:, BLK:2 * BLK], ps_b[:, 2 * BLK:3 * BLK], ACT.Tanh,
                                 scale=0.5 / WSCALE).then_inc(tanh_done, 1)
                if prev:
                    wait(act, yn_by_channel, i)
                    wait(act, set_done, 2)
                    for c in range(DC):
                        a.activation(yn[:, c * BLK:(c + 1) * BLK], ps_t[:, c * BLK:(c + 1) * BLK], ACT.Identity,
                                     scale=ln_gb[:, 0, c:c + 1], bias=ln_gb[:, 1, c:c + 1]).then_inc(affine, 1)
                if prev2:
                    wait(act, rstd_x, i - 1)
                    wait(act, x1_by_channel, i - 3)
                    wait(act, row_lo, i - 3)
                    wait(act, x1_kept[u], 16 * (j - 1))
                    for s in range(S):
                        last = a.activation(x1_new[u][:, s * D:(s + 1) * D], x_tok[u][:, s * D:(s + 1) * D],
                                            ACT.Identity, scale=rs_x[:, 1, s:s + 1], bias=rs_x[:, 2, s:s + 1])
                    last.then_inc(x1_done, 1)
                if prev:
                    wait(act, z_done, i)
                    wait(act, out_projected, i - 1)
                    a.activation(z_hi[:, :, :], yn[:, :].rearrange("p (c t) -> p c t", c=DC),
                                 ACT.Copy).then_inc(zhi_done, 1)
                if now:
                    wait(act, projected, 2 * i + 2)
                    a.activation(gate[u][:, 0:BLK], ps_a[:, 2 * BLK:3 * BLK], ACT.Tanh,
                                 scale=0.5 / WSCALE).then_inc(tanh_done, 1)
                    if not (isinstance(i, int) and i == NB - 1):
                        split_x(i + 1, 1 - u, j + u + 1)
                if prev2:
                    wait(act, x1_by_channel, i - 1)
                    wait(act, routed, i - 2)
                    a.activation(x1T[:, :], ps_t[:, :], ACT.Copy).then_inc(x1T_done, 1)
                    wait(act, scattered[u], 128 * (j - 1))
                    wait(act, set_done, 1)
                    a.activation(row[u][:, :, :].bitcast(F16)[:, :, 0:D],
                                 x1_new[u][:, :].rearrange("p (s d) -> p s d", s=S),
                                 ACT.Copy).then_inc(row_hi, 1)
                if now:
                    wait(act, wf_in, 16 * (i + 1))
                    a.activation(wf32[:, :], wf32[:, :], ACT.Copy, scale=WSCALE).then_inc(wf_scaled, 1)
                    wait(act, wf_scaled, i + 1)
                    a.activation(wf16[:, bass.ds(j * 4 * DC * HID + u * 2 * DC * HID, DC * HID)], wf32[:, :],
                                 ACT.Copy).then_inc(wf_hi_done, 1)
                    wait(act, rstd_y, i + 1)
                    wait(act, zlo_done, i)
                    for s in range(S):
                        last = a.activation(yn[:, s * D:(s + 1) * D], yT[:, s * D:(s + 1) * D], ACT.Identity,
                                            scale=rs_y[:, 1, s:s + 1], bias=rs_y[:, 2, s:s + 1])
                    last.then_inc(y_normed, 1)

            pipeline(act, step)

        @block.gpsimd
        def _(pool):
            g = nc.gpsimd
            pool.wait_ge(par_in, 16 * N_PAR)
            pool.wait_ge(set_done, 1)
            zeros_set = (set_done, 1)

            def split_x(b, u):
                wait(pool, x_hi, b + 1)
                wait(pool, projected, 2 * b)
                g.tensor_tensor(xT_lo[:, :, :], xT32[u][:, :].rearrange("p (c t) -> p c t", c=DC),
                                xT_hi[:, :, :], ALU.subtract).then_inc(x_lo, 1)

            def rstd(mv, rs, stepped, done, n):
                g.tensor_tensor(rs[:, 2, :], mv[:, :, 0], minus_one[:, :], ALU.mult)
                g.tensor_tensor(rs[:, 0, :], mv[:, :, 1], eps[:, :], ALU.add).then_inc(stepped, 1)
                wait(pool, stepped, 2 * n + 1)
                g.tensor_tensor(rs[:, 1, :], rs[:, 0, :], half_pow[:, :], ALU.pow).then_inc(stepped, 1)
                wait(pool, stepped, 2 * n + 2)
                g.tensor_tensor(rs[:, 2, :], rs[:, 2, :], rs[:, 1, :], ALU.mult).then_inc(done, 1)

            g.tensor_copy(token[:, :], token0[:, :]).then_inc(token_next, 1)
            split_x(0, 0)

            def step(j, u, now, prev, prev2):
                i = 2 * j + u
                b = i - 2
                if now and not (isinstance(i, int) and i == NB - 1):
                    split_x(i + 1, 1 - u)
                if now:
                    wait(pool, stats_y, i + 1)
                    wait(pool, y_normed, i)
                    rstd(mv_y, rs_y, rstd_y_step, rstd_y, i)
                    wait(pool, wf_hi_done, i + 1)
                    base = j * 4 * DC * HID + u * 2 * DC * HID
                    g.tensor_tensor(wf16[:, bass.ds(base + DC * HID, DC * HID)], wf32[:, :],
                                    wf16[:, bass.ds(base, DC * HID)], ALU.subtract).then_inc(wf_lo_done, 1)
                if prev2:
                    wait(pool, chosen_done, b + 1, beside=zeros_set)
                    g.tensor_copy(m8[:, bass.ds(b * S * E, S * E)],
                                  m8_new[:, :, :].rearrange("p s e -> p (s e)")).then_inc(top_kept, 1)
                    wait(pool, row_hi, b + 1, beside=zeros_set)
                    wait(pool, token_next, b + 1, beside=zeros_set)
                    g.tensor_copy(row[u][:, :, META], token[:, :]).then_inc(meta_done, 1)
                    g.tensor_copy(row[u][:, :, META + 1], chosen[:, 1, :]).then_inc(meta_done, 1)
                    wait(pool, meta_done, 2 * b + 2)
                    g.tensor_tensor(token[:, :], token[:, :], blk[:, :], ALU.add).then_inc(token_next, 1)
                if prev:
                    wait(pool, stats_x, i)
                    wait(pool, x1_done, i - 1)
                    rstd(mv_x, rs_x, rstd_x_step, rstd_x, i - 1)
                if prev2:
                    wait(pool, slots_done, b + 1, beside=zeros_set)
                    wait(pool, row_lo, b + 1, beside=zeros_set)
                    for k in range(2):
                        for s in range(S):
                            g.indirect_dma_start(region, bass.IndirectOffsetOnAxis(slot[u][:, k, s:s + 1], 0),
                                                 row[u][:, s, :].bitcast(F16), None).then_inc(scattered[u], 16)

            pipeline(pool, step)
            for u in range(2):
                pool.wait_ge(scattered[u], 128 * NB // 2)


def build_experts(nc, io, keep):
    wf16, m8, count_acc, tri_ones, cw = (keep[n] for n in ("wf16", "m8", "count_acc", "tri_ones", "cw"))
    region, outputs = io["region"], io["outputs"]
    NT = NB * S
    WE = 4 * DC * HID
    with ExitStack() as ctx:
        def sb(name, shape, dt):
            return ctx.enter_context(nc.sbuf_tensor(name, shape, dt))

        def psum(name, shape, dt):
            return ctx.enter_context(nc.psum_tensor(name, shape, dt))

        def sem(name):
            return ctx.enter_context(nc.semaphore(name))

        tile_iota = sb("tile_iota", [P, TILES], F32)
        region_base = sb("region_base_2", [P, E], F32)
        ones_e = sb("ones_e", [P, E], F32)
        slots_of = sb("slots_of", [P, E], F32)
        tiles_i = sb("tiles_i", [P, E], I32)
        tiles_of = sb("tiles_of", [P, E], F32)
        tiles_to = sb("tiles_to", [P, E], F32)
        skip_rows = sb("skip_rows", [P, E], F32)
        tail_f = sb("tail_f", [P, E], F32)
        tail_i = sb("tail_i", [P, E], I32)
        expert_f = sb("expert_f", [P, TILES], F32)
        offset_f = sb("offset_f", [P, TILES], F32)
        skipped = sb("skipped", [P, TILES], F32)
        expert_i = sb("expert_i", [P, TILES], I32)
        offset_i = sb("offset_i", [P, TILES], I32)
        blank = sb("blank", [P, TS, ROWF], F32)
        dif = sb("dif", [P, NT, E], F32)
        prob = sb("prob", [P, NT, 2], F32)
        total = sb("total", [P, NT], F32)
        inv = sb("inv", [P, NT], F32)
        ident16 = sb("ident16", [P, P], F16)
        b1 = sb("b1", [P, E * HC], F32)
        b2 = sb("b2", [P, E * D], F32)
        rows = [sb(f"rows_{u}", [P, TS, ROWF], F32) for u in range(2)]
        xT = [sb(f"xT_{u}", [P, 2 * DC * TILE], F16) for u in range(2)]
        h = [sb(f"h_{u}", [P, HC * TILE], F32) for u in range(2)]
        h_hi = [sb(f"h_hi_{u}", [P, HC * TILE], F16) for u in range(2)]
        h_lo = [sb(f"h_lo_{u}", [P, HC * TILE], F16) for u in range(2)]
        y_out = [sb(f"y_out_{u}", [P, TS * D], F32) for u in range(2)]
        is_second = [sb(f"is_second_{u}", [P, TS], F32) for u in range(2)]
        token = [sb(f"token_of_{u}", [P, TS], F32) for u in range(2)]
        dest_f = sb("dest_f", [P, TS], F32)
        dest = [sb(f"dest_{u}", [P, TS], U32) for u in range(2)]

        ps_x = psum("ps_x", [P, 2 * DC * TILE], F16)
        ps_h = [psum(f"ps_h_{u}", [P, HC * TILE], F32) for u in range(2)]
        ps_y = [psum(f"ps_y_{u}", [P, TS * D], F32) for u in range(2)]
        ps_n = psum("ps_n", [P, E], F32)

        par_in = sem("par_in_2")
        rows_in = [sem("rows_in_0"), sem("rows_in_1")]
        blanked = sem("blanked")
        scattered = [sem("y_scattered_0"), sem("y_scattered_1")]
        zeroed = sem("zeroed")
        total_slots = sem("total_slots")
        table_step = sem("table_step")
        table_done = sem("table_done")
        dif_done = sem("dif_done")
        exp_done = sem("exp_done")
        cw_step = sem("cw_step")
        x_transposed = sem("x_transposed")
        x_copied = sem("x_copied")
        hidden = sem("hidden")
        relu_done = sem("relu_done")
        h_hi_done = sem("h_hi_done")
        h_lo_done = sem("h_lo_done")
        projected = sem("y_projected")
        second_done = sem("second_done")
        dest_f_done = sem("dest_f_done")
        dest_done = sem("dest_done")
        y_ready = sem("y_ready")

        N_PAR = 5

        def pipeline(eng, step):
            for t in range(4):
                step(t // 2, t % 2, True, True)
            with eng.Fori(2, TILES // 2) as j:
                for u in range(2):
                    step(j, u, True, True)
            step(TILES // 2, 0, True, False)
            step(TILES // 2, 1, False, False)

        assert TILES % 2 == 1
        block = ctx.enter_context(nc.Block())

        @block.sync
        def _(sp):
            for dst, src in ((tile_iota[:, :], io["tile_iota"]), (region_base[:, :], io["region_base"]),
                             (ident16[:, :], io["ident16"]), (b1[:, :], io["b1"]),
                             (b2[:, :], io["b2"].partition_broadcast(P))):
                sp.dma_start(dst, src).then_inc(par_in, 16)
            sp.wait_ge(table_done, 1)
            for e in range(E):
                first = sp.value_load(tail_i[0:1, e:e + 1], min_val=0, max_val=E * REGION - TILE)
                sp.dma_start(region[bass.ds(first, TILE), :].rearrange("(s p) w -> p s w", p=P),
                             blank[:, :, :].bitcast(F16)).then_inc(blanked, 16)
            sp.dma_start(region[E * REGION:E * REGION + TILE, :].rearrange("(s p) w -> p s w", p=P),
                         blank[:, :, :].bitcast(F16)).then_inc(blanked, 16)
            sp.wait_ge(blanked, 16 * (E + 1))

            def load(j, u):
                t = 2 * j + u
                wait(sp, x_transposed, t - 1)
                wait(sp, second_done, t - 1)
                first = sp.value_load(offset_i[0:1, bass.ds(t, 1)], min_val=0, max_val=E * REGION)
                sp.dma_start(rows[u][:, :, :].bitcast(F16),
                             region[bass.ds(first, TILE), :].rearrange("(s p) w -> p s w", p=P)
                             ).then_inc(rows_in[u], 16)

            for t in range(4):
                load(t // 2, t % 2)
            with sp.Fori(2, TILES // 2) as j:
                for u in range(2):
                    load(j, u)
            load(TILES // 2, 0)

        @block.tensor
        def _(pe):
            nc.tensor.matmul(ps_n[:, :], tri_ones[:, 1, :], count_acc[:, :], start=True,
                             stop=True).then_inc(total_slots, 1)
            pe.wait_ge(par_in, 16 * N_PAR)

            def transpose_rows(t, u, loads):
                wait(pe, rows_in[u], 16 * loads)
                wait(pe, x_copied, t)
                src = rows[u][:, :, :].bitcast(F16)
                for half in range(2):
                    for k in range(DC):
                        for s in range(TS):
                            at = (half * DC + k) * TILE + s * P
                            last = nc.tensor.transpose(ps_x[:, at:at + P],
                                                       src[:, s, half * D + k * P:half * D + (k + 1) * P],
                                                       ident16[:, :])
                last.then_inc(x_transposed, 1)

            transpose_rows(0, 0, 1)

            def step(j, u, now, after):
                t = 2 * j + u
                if now:
                    e = pe.value_load(expert_i[0:1, bass.ds(t, 1)], min_val=0, max_val=E - 1)
                    wait(pe, x_copied, t + 1)
                    wait(pe, relu_done, 2 * (t - 1))
                    for c in range(HC):
                        m = 0
                        for k in range(DC):
                            for wl, xl in ((0, 0), (1, 0), (0, 1)):
                                last = nc.tensor.matmul(
                                    ps_h[u][:, c * TILE:(c + 1) * TILE],
                                    wf16[:, bass.ds(e * WE + (wl * DC + k) * HID + c * P, P)],
                                    xT[u][:, (xl * DC + k) * TILE:(xl * DC + k + 1) * TILE],
                                    start=(m == 0), stop=(m == 3 * DC - 1))
                                m += 1
                        if c % 2:
                            last.then_inc(hidden, 1)
                if after:
                    transpose_rows(t + 1, 1 - u, j + u + 1)
                if not (isinstance(t, int) and t == 0):
                    e = pe.value_load(expert_i[0:1, bass.ds(t - 1, 1)], min_val=0, max_val=E - 1)
                    wait(pe, h_lo_done, t)
                    wait(pe, y_ready, t - 2)
                    for s in range(TS):
                        m = 0
                        for k in range(HC):
                            for hl, wl in ((h_hi, 0), (h_lo, 0), (h_hi, 1)):
                                last = nc.tensor.matmul(
                                    ps_y[1 - u][:, s * D:(s + 1) * D],
                                    hl[1 - u][:, k * TILE + s * P:k * TILE + (s + 1) * P],
                                    wf16[:, bass.ds(e * WE + 2 * DC * HID + (wl * HC + k) * D, D)],
                                    start=(m == 0), stop=(m == 3 * HC - 1))
                                m += 1
                    last.then_inc(projected, 1)

            pipeline(pe, step)

        @block.vector
        def _(dve):
            v = nc.vector
            steps = [0]

            def link(ins):
                steps[0] += 1
                ins.then_inc(table_step, 1)
                dve.wait_ge(table_step, steps[0])

            v.memset(ones_e[:, :], 1.0)
            v.memset(blank[:, :, :], 0.0)
            v.memset(expert_f[:, :], 0.0)
            dve.wait_ge(total_slots, 1)
            link(v.tensor_copy(slots_of[:, :], ps_n[:, :]))
            v.memset(blank[:, :, META], NO_TOKEN)
            v.memset(blank[:, :, META + 1], -1.0)
            link(v.tensor_scalar(tiles_i[:, :], slots_of[:, :], float(TILE - 1), None, ALU.add))
            link(v.tensor_scalar(tiles_i[:, :], tiles_i[:, :], TILE.bit_length() - 1, None, ALU.arith_shift_right))
            link(v.tensor_copy(tiles_of[:, :], tiles_i[:, :]))
            link(v.tensor_tensor_scan(tiles_to[:, :], ones_e[:, :], tiles_of[:, :], 0.0, ALU.mult, ALU.add))
            link(v.tensor_scalar(skip_rows[:, :], tiles_of[:, :], -float(TILE), float(REGION), ALU.mult, ALU.add))
            dve.wait_ge(par_in, 16 * N_PAR)
            v.tensor_tensor(tail_f[:, :], region_base[:, :], slots_of[:, :], ALU.add)
            link(v.tensor_scalar(offset_f[:, :], tile_iota[:, :], float(TILE), None, ALU.mult))
            v.tensor_copy(tail_i[:, :], tail_f[:, :])
            for e in range(E):
                link(v.tensor_scalar(skipped[:, :], tile_iota[:, :], tiles_to[:, e:e + 1], skip_rows[:, e:e + 1],
                                     ALU.is_ge, ALU.mult))
                v.scalar_tensor_tensor(out=expert_f[:, :], in0=tile_iota[:, :], scalar=tiles_to[:, e:e + 1],
                                       in1=expert_f[:, :], op0=ALU.is_ge, op1=ALU.add)
                link(v.tensor_tensor(offset_f[:, :], offset_f[:, :], skipped[:, :], ALU.add))
            v.tensor_scalar(offset_i[:, :], offset_f[:, :], float(E * REGION), None, ALU.min)
            link(v.tensor_scalar(expert_f[:, :], expert_f[:, :], float(E - 1), None, ALU.min))
            v.tensor_copy(expert_i[:, :], expert_f[:, :]).then_inc(table_done, 1)

            def take_x(t, u):
                wait(dve, x_transposed, t + 1)
                wait(dve, hidden, 2 * (t - 1))
                v.tensor_copy(xT[u][:, :], ps_x[:, :]).then_inc(x_copied, 1)

            take_x(0, 0)
            m8v = m8[:, :].rearrange("p (t e) -> p t e", e=E)
            v.tensor_tensor(dif[:, :, :], m8v, m8v[:, :, 0:1].broadcast_to([P, NT, E]), ALU.subtract).then_inc(dif_done, 1)
            dve.wait_ge(exp_done, 1)
            link(v.tensor_reduce(total[:, :], dif[:, :, :], AX_X, ALU.add))
            link(v.reciprocal(inv[:, :], total[:, :]))
            link(v.tensor_tensor(prob[:, :, :], dif[:, :, 0:2], inv[:, :].unsqueeze(2).broadcast_to([P, NT, 2]), ALU.mult))
            link(v.tensor_tensor(total[:, :], prob[:, :, 0], prob[:, :, 1], ALU.add))
            link(v.tensor_scalar(total[:, :], total[:, :], 1e-8, 2.0, ALU.add, ALU.mult))
            link(v.reciprocal(inv[:, :], total[:, :]))
            link(v.tensor_tensor(cw[:, :].rearrange("p (t k) -> p t k", k=2), prob[:, :, :],
                                 inv[:, :].unsqueeze(2).broadcast_to([P, NT, 2]), ALU.mult))

            def step(j, u, now, after):
                t = 2 * j + u
                if now:
                    wait(dve, rows_in[u], 16 * (j + 1))
                    wait(dve, dest_f_done, t - 1)
                    v.tensor_copy(token[u][:, :], rows[u][:, :, META])
                    v.tensor_scalar(is_second[u][:, :], rows[u][:, :, META + 1], expert_f[:, bass.ds(t, 1)],
                                    float(TOKENS), ALU.is_equal, ALU.mult).then_inc(second_done, 1)
                if after:
                    take_x(t + 1, 1 - u)
                if now:
                    wait(dve, h_hi_done, t + 1)
                    wait(dve, projected, t - 1)
                    v.tensor_tensor(h_lo[u][:, :], h[u][:, :], h_hi[u][:, :], ALU.subtract).then_inc(h_lo_done, 1)
                if not (isinstance(t, int) and t == 0):
                    e = dve.value_load(expert_i[0:1, bass.ds(t - 1, 1)], min_val=0, max_val=E - 1)
                    wait(dve, projected, t)
                    if not (isinstance(t, int) and t < 3):
                        wait(dve, scattered[1 - u], 32 * (j + u - 1))
                    v.scalar_tensor_tensor(out=y_out[1 - u][:, :].rearrange("p (s d) -> p s d", s=TS),
                                           in0=ps_y[1 - u][:, :].rearrange("p (s d) -> p s d", s=TS),
                                           scalar=1.0 / WSCALE,
                                           in1=b2[:, bass.ds(e * D, D)].unsqueeze(1).broadcast_to([P, TS, D]),
                                           op0=ALU.mult, op1=ALU.add).then_inc(y_ready, 1)

            pipeline(dve, step)

        @block.scalar
        def _(act):
            a = nc.scalar
            act.wait_ge(dif_done, 1)
            a.activation(dif[:, :, :], dif[:, :, :], ACT.Exp).then_inc(exp_done, 1)
            act.wait_ge(table_done, 1)

            def step(j, u, now, after):
                t = 2 * j + u
                if not now:
                    return
                e = act.value_load(expert_i[0:1, bass.ds(t, 1)], min_val=0, max_val=E - 1)
                wait(act, h_lo_done, t - 1)
                for c in range(HC):
                    if c % 2 == 0:
                        wait(act, hidden, 2 * t + c // 2 + 1)
                    last = a.activation(h[u][:, c * TILE:(c + 1) * TILE], ps_h[u][:, c * TILE:(c + 1) * TILE],
                                        ACT.Relu, scale=1.0 / WSCALE, bias=b1[:, bass.ds(e * HC + c, 1)])
                    if c % 2:
                        last.then_inc(relu_done, 1)
                wait(act, relu_done, 2 * t + 2)
                wait(act, projected, t - 1)
                a.activation(h_hi[u][:, :], h[u][:, :], ACT.Copy).then_inc(h_hi_done, 1)

            pipeline(act, step)

        @block.gpsimd
        def _(pool):
            pool.wait_ge(table_done, 1)
            table_set = (table_done, 1)

            def step(j, u, now, after):
                t = 2 * j + u
                if isinstance(t, int) and t == 0:
                    return
                wait(pool, second_done, t)
                if not (isinstance(t, int) and t < 3):
                    wait(pool, scattered[1 - u], 32 * (j + u - 1))
                nc.gpsimd.tensor_tensor(dest_f[:, :], is_second[1 - u][:, :], token[1 - u][:, :],
                                        ALU.add).then_inc(dest_f_done, 1)
                wait(pool, dest_f_done, t, beside=table_set)
                nc.gpsimd.tensor_copy(dest[1 - u][:, :], dest_f[:, :]).then_inc(dest_done, 1)
                wait(pool, dest_done, t, beside=table_set)
                wait(pool, y_ready, t, beside=table_set)
                for s in range(TS):
                    nc.gpsimd.indirect_dma_start(outputs, bass.IndirectOffsetOnAxis(dest[1 - u][:, s:s + 1], 0),
                                                 y_out[1 - u][:, s * D:(s + 1) * D], None,
                                                 bounds_check=2 * TOKENS - 1,
                                                 oob_is_err=False).then_inc(scattered[1 - u], 16)

            pipeline(pool, step)
            pool.wait_ge(scattered[0], 32 * (TILES // 2 + 1))
            pool.wait_ge(scattered[1], 32 * (TILES // 2))


def build_combine(nc, io, keep):
    x1, cw = keep["x1"], keep["cw"]
    y2 = io["outputs"].rearrange("(k b s p) d -> k b p s d", k=2, b=NB, p=P)
    out = io["out"].rearrange("(b s p) d -> b p s d", b=NB, p=P)
    N_BUF = 2
    with ExitStack() as ctx:
        def sb(name, shape, dt):
            return ctx.enter_context(nc.sbuf_tensor(name, shape, dt))

        def sem(name):
            return ctx.enter_context(nc.semaphore(name))

        first = [sb(f"first_{u}", [P, S, D], F32) for u in range(N_BUF)]
        second = [sb(f"second_{u}", [P, S, D], F32) for u in range(N_BUF)]
        normed = [sb(f"normed_{u}", [P, S, D], F32) for u in range(N_BUF)]
        half_pow = sb("half_pow_2", [P, S], F32)
        eps = sb("eps_2", [P, S], F32)
        minus_one = sb("minus_one_2", [P, S], F32)
        bn = sb("bn", [P, S, 6], F32)
        mv = sb("mv", [P, S, 2], F32)
        rs = sb("rs", [P, 3, S], F32)
        first_in = [sem("first_in_0"), sem("first_in_1")]
        second_in = [sem("second_in_0"), sem("second_in_1")]
        stored = [sem("stored_0"), sem("stored_1")]
        set_done = sem("set_done_2")
        added = sem("added")
        added_2 = sem("added_2")
        bn_done = sem("bn_done")
        stats = sem("stats")
        rstd_step = sem("rstd_step")
        rstd = sem("rstd")
        norm_done = sem("norm_done")

        def blocks(eng, step):
            for i in range(4):
                step(i // 2, i % 2)
            with eng.Fori(2, NB // 2) as j:
                for u in range(2):
                    step(j, u)

        block = ctx.enter_context(nc.Block())

        @block.sync
        def _(sp):
            def step(j, u):
                i = 2 * j + u
                wait(sp, norm_done, i - 1)
                sp.dma_start(first[u][:, :, :], y2[0, i]).then_inc(first_in[u], 16)
                sp.dma_start(second[u][:, :, :], y2[1, i]).then_inc(second_in[u], 16)

            blocks(sp, step)

        @block.vector
        def _(dve):
            v = nc.vector
            v.memset(eps[:, :], LN_EPS / 4)
            v.memset(minus_one[:, :], -1.0)
            v.memset(half_pow[:, :], -0.5).then_inc(set_done, 1)

            def step(j, u):
                i = 2 * j + u
                wait(dve, first_in[u], 16 * (j + 1))
                wait(dve, second_in[u], 16 * (j + 1))
                for s in range(S):
                    last = v.scalar_tensor_tensor(out=first[u][:, s, :], in0=first[u][:, s, :],
                                                  scalar=cw[:, bass.ds((i * S + s) * 2, 1)],
                                                  in1=x1[:, bass.ds((i * S + s) * D, D)],
                                                  op0=ALU.mult, op1=ALU.add)
                last.then_inc(added, 1)
                wait(dve, added, i + 1)
                for s in range(S):
                    last = v.scalar_tensor_tensor(out=first[u][:, s, :], in0=second[u][:, s, :],
                                                  scalar=cw[:, bass.ds((i * S + s) * 2 + 1, 1)],
                                                  in1=first[u][:, s, :], op0=ALU.mult, op1=ALU.add)
                last.then_inc(added_2, 1)
                wait(dve, added_2, i + 1)
                for s in range(S):
                    last = v.bn_stats(bn[:, s, :], first[u][:, s, :])
                last.then_inc(bn_done, 1)
                wait(dve, bn_done, i + 1, beside=(set_done, 1))
                wait(dve, rstd, i)
                for s in range(S):
                    last = v.bn_aggr(mv[:, s, :], bn[:, s, :])
                last.then_inc(stats, 1)

            blocks(dve, step)

        @block.gpsimd
        def _(pool):
            g = nc.gpsimd
            pool.wait_ge(set_done, 1)

            def step(j, u):
                i = 2 * j + u
                wait(pool, stats, i + 1)
                wait(pool, norm_done, i)
                g.tensor_tensor(rs[:, 2, :], mv[:, :, 0], minus_one[:, :], ALU.mult)
                g.tensor_tensor(rs[:, 0, :], mv[:, :, 1], eps[:, :], ALU.add).then_inc(rstd_step, 1)
                wait(pool, rstd_step, 2 * i + 1)
                g.tensor_tensor(rs[:, 1, :], rs[:, 0, :], half_pow[:, :], ALU.pow).then_inc(rstd_step, 1)
                wait(pool, rstd_step, 2 * i + 2)
                g.tensor_tensor(rs[:, 2, :], rs[:, 2, :], rs[:, 1, :], ALU.mult).then_inc(rstd, 1)

            blocks(pool, step)

        @block.scalar
        def _(act):
            def step(j, u):
                i = 2 * j + u
                wait(act, rstd, i + 1)
                wait(act, stored[u], 16 * j)
                for s in range(S):
                    last = nc.scalar.activation(normed[u][:, s, :], first[u][:, s, :], ACT.Identity,
                                                scale=rs[:, 1, s:s + 1], bias=rs[:, 2, s:s + 1])
                last.then_inc(norm_done, 1)
                wait(act, norm_done, i + 1)
                act.dma_start(out[i], normed[u][:, :, :]).then_inc(stored[u], 16)

            blocks(act, step)
            for u in range(2):
                act.wait_ge(stored[u], 16 * NB // 2)


def build(nc, io):
    io["region"] = nc.dram_tensor("region", [E * REGION + TILE, ROW], F16, kind="Internal").ap()
    io["outputs"] = nc.dram_tensor("outputs", [2 * TOKENS, D], F32, kind="Internal").ap()
    with ExitStack() as ctx:
        keep = {
            "x1": ctx.enter_context(nc.sbuf_tensor("x1", [P, NB * S * D], F32)),
            "wf16": ctx.enter_context(nc.sbuf_tensor("wf16", [P, E * 4 * DC * HID], F16)),
            "m8": ctx.enter_context(nc.sbuf_tensor("m8", [P, NB * S * E], F32)),
            "count_acc": ctx.enter_context(nc.sbuf_tensor("count_acc", [P, E], F16)),
            "tri_ones": ctx.enter_context(nc.sbuf_tensor("tri_ones", [P, 2, P], F16)),
        }
        keep["cw"] = keep["m8"][:, 0:NB * S * 2]
        build_attend(nc, io, keep)
        build_experts(nc, io, keep)
        build_combine(nc, io, keep)


def kernel(**inputs):
    import numpy as np
    import concourse.bacc as bacc
    from concourse.bass_utils import run_bass_kernel_spmd

    x = inputs["L0_attn_x"].reshape(TOKENS, D)
    arrays = {
        "xT": x.reshape(NB, BLK, DC, P).transpose(0, 3, 2, 1).reshape(NB, P, DC * BLK),
        "x_tok": x.reshape(NB, S, P, D).transpose(0, 2, 1, 3),
        "wa": np.stack([inputs[f"L0_attn_{n}"].T.reshape(DC, P, D) for n in ("Wq", "Wv", "Wg", "Wo")], axis=2),
        "wf": np.stack([inputs["L0_ffn_W1"].reshape(E, DC, P, HID).transpose(0, 2, 1, 3).reshape(E, P, DC * HID),
                        inputs["L0_ffn_W2"].reshape(E, HC, P, D).transpose(0, 2, 1, 3).reshape(E, P, HC * D)],
                       axis=1).reshape(2 * E, P, DC * HID),
        "b1": inputs["L0_ffn_b1"].reshape(E * HC, P).T,
        "b2": inputs["L0_ffn_b2"].reshape(E * D),
        "gate_w": inputs["L0_ffn_gate_W"].reshape(DC, P, E).transpose(1, 0, 2),
        "ln_gb": np.stack([inputs["L0_attn_ln_g"].reshape(DC, P), inputs["L0_attn_ln_b"].reshape(DC, P)]).transpose(2, 0, 1),
        "lam": np.repeat(inputs["L0_attn_decay"][:, 1, 0], D // 16).reshape(DC, P).T,
        "ident": np.eye(P, dtype=np.float32),
        "ident16": np.eye(P, dtype=np.float16),
        "tri_ones": np.stack([np.triu(np.ones((P, P), np.float16), 1), np.ones((P, P), np.float16)], axis=1),
        "iota_e": np.tile(np.arange(E, dtype=np.float32), (P, 1)),
        "region_base": np.tile(np.arange(E, dtype=np.float32) * REGION, (P, 1)),
        "tile_iota": np.tile(np.arange(TILES, dtype=np.float32), (P, 1)),
        "token0": (np.arange(P)[:, None] + P * np.arange(S)[None, :]).astype(np.float32),
        "keep_state": np.tile((np.arange(NB + 1) % BLOCKS_PER_SEQ != 0).astype(np.float32), (P, 1)),
    }
    arrays = {n: np.ascontiguousarray(a) for n, a in arrays.items()}
    nc = bacc.Bacc("TRN2", target_bir_lowering=False, num_devices=1)
    io = {n: nc.dram_tensor(n + "_in", a.shape, mybir.dt.from_np(a.dtype), kind="ExternalInput").ap()
          for n, a in arrays.items()}
    io["out"] = nc.dram_tensor("out", [TOKENS, D], F32, kind="ExternalOutput").ap()
    build(nc, io)
    r = run_bass_kernel_spmd(nc, [{n + "_in": a for n, a in arrays.items()}], core_ids=[0])
    return r.results[0]["out"].reshape(inputs["L0_attn_x"].shape)
```

```python
from contextlib import ExitStack

import concourse.bass as bass
from concourse import mybir

F32 = mybir.dt.float32
F16 = mybir.dt.float16
U32 = mybir.dt.uint32
I32 = mybir.dt.int32
ALU = mybir.AluOpType
ACT = mybir.ActivationFunctionType
AX_X = mybir.AxisListType.X

P = 128
D = 256
DC = D // P
E = 8
HID = 512
HC = HID // P
TOKENS = 8192
BLK = 512
NB = TOKENS // BLK
BLOCKS_PER_SEQ = 8
S = BLK // P
TILE = 256
TS = TILE // P
REGION = TOKENS + TILE
TILES = (2 * TOKENS + E * (TILE - 1)) // TILE
ROW = 528
ROWF = ROW // 2
META = 2 * D // 2
NO_TOKEN = 20000.0
WSCALE = 64.0
LN_EPS = 1e-05
W_Q, W_V, W_G, W_O = range(4)


def wait(eng, sem, value, beside=None):
    if not isinstance(value, int) or value > 0:
        if beside is not None and not isinstance(value, int):
            eng.wait_ge(*beside)
        eng.wait_ge(sem, value)


def build_attend(nc, io, keep):
    x1, wf16, m8, cw = keep["x1"], keep["wf16"], keep["m8"], keep["cw"]
    expert_f, expert_i, offset_i = keep["expert_f"], keep["expert_i"], keep["offset_i"]
    region = io["region"]
    with ExitStack() as ctx:
        def sb(name, shape, dt):
            return ctx.enter_context(nc.sbuf_tensor(name, shape, dt))

        def sem(name):
            return ctx.enter_context(nc.semaphore(name))

        ident = sb("ident", [P, P], F32)
        tri_ones = sb("tri_ones", [P, 2, P], F16)
        count_acc = sb("count_acc", [P, E], F16)
        iota_e = sb("iota_e", [P, E], F32)
        region_base = sb("region_base", [P, E], F32)
        token0 = sb("token0", [P, S], F32)
        tile_iota = sb("tile_iota", [P, TILES], F32)
        keep_state = sb("keep_state", [P, NB + 1], F32)
        half_pow = sb("half_pow", [P, S], F32)
        eps = sb("eps", [P, S], F32)
        minus_one = sb("minus_one", [P, S], F32)
        blk = sb("blk", [P, S], F32)
        ones_e = sb("ones_e", [P, E], F32)
        lam = sb("lam", [P, DC], F32)
        ln_gb = sb("ln_gb", [P, 2, DC], F32)
        gate_w = sb("gate_w", [P, DC, E], F32)
        wa_hi = sb("wa_hi", [P, 4, DC, D], F16)
        wa_lo = sb("wa_lo", [P, 4, DC, D], F16)
        xT32 = [sb(f"xT32_{u}", [P, DC * BLK], F32) for u in range(2)]
        xT_hi = sb("xT_hi", [P, DC, BLK], F16)
        xT_lo = sb("xT_lo", [P, DC, BLK], F16)
        x_tok = [sb(f"x_tok_{u}", [P, S * D], F32) for u in range(2)]
        carry = sb("carry", [P, DC], F32)
        y = sb("y", [P, DC, BLK], F32)
        gate = [sb(f"gate_{u}", [P, DC * BLK], F32) for u in range(2)]
        yn = sb("yn", [P, DC * BLK], F32)
        wa32 = [t[:, :].rearrange("p (w d) -> p w d", w=4) for t in (gate[1], yn)]
        z_hi = sb("z_hi", [P, DC, BLK], F16)
        z_lo = sb("z_lo", [P, DC, BLK], F16)
        row = [sb(f"row_{u}", [P, S, ROWF], F32) for u in range(2)]
        x1_new = [sb(f"x1_new_{u}", [P, S * D], F32) for u in range(2)]
        x1T = sb("x1T", [P, DC * BLK], F32)
        wf32 = sb("wf32", [P, DC * HID], F32)
        bn_y = sb("bn_y", [P, S, 6], F32)
        mv_y = sb("mv_y", [P, S, 2], F32)
        rs_y = sb("rs_y", [P, 3, S], F32)
        bn_x = sb("bn_x", [P, S, 6], F32)
        mv_x = sb("mv_x", [P, S, 2], F32)
        rs_x = sb("rs_x", [P, 3, S], F32)
        m8_new = sb("m8_new", [P, S, E], F32)
        i8 = sb("i8", [P, S, E], U32)
        chosen = sb("chosen", [P, 2, S], F32)
        onehot = sb("onehot", [P, 2, S, E], F32)
        mask = sb("mask", [P, S, E], F16)
        block_sum = sb("block_sum", [P, E], F32)
        position = sb("position", [P, S, E], F32)
        picked = sb("picked", [P, 2, S, E], F32)
        slot = [sb(f"slot_{u}", [P, 2, S], U32) for u in range(2)]
        token = sb("token", [P, S], F32)

        ps_a = ctx.enter_context(nc.psum_tensor("ps_a", [P, 3 * BLK], F32))
        ps_b = ctx.enter_context(nc.psum_tensor("ps_b", [P, 3 * BLK], F32))
        ps_t = ctx.enter_context(nc.psum_tensor("ps_t", [P, 2 * BLK], F32))
        vqg = [ps_a, ps_b]
        ps_n = ps_t[:, 0:E]
        yT = ps_a[:, 0:2 * BLK]
        ps_logits = ps_a[:, 2 * BLK:2 * BLK + S * E]
        ps_pos = ps_a[:, 2 * BLK + 64:2 * BLK + 64 + S * E]

        par_in = sem("par_in")
        wa_in = [sem("wa_in_0"), sem("wa_in_1")]
        xT_in = [sem("xT_in_0"), sem("xT_in_1")]
        xtok_in = [sem("xtok_in_0"), sem("xtok_in_1")]
        wf_in = sem("wf_in")
        x1_kept = [sem("x1_kept_0"), sem("x1_kept_1")]
        scattered = [sem("scattered_0"), sem("scattered_1")]
        set_done = sem("set_done")
        wa_hi_done = sem("wa_hi_done")
        wa_lo_done = sem("wa_lo_done")
        x_hi = sem("x_hi")
        x_lo = sem("x_lo")
        projected = sem("projected")
        tanh_done = sem("tanh_done")
        scanned = sem("scanned")
        gated = sem("gated")
        y_done = sem("y_done")
        carried = sem("carried")
        y_by_token = sem("y_by_token")
        bn_y_done = sem("bn_y_done")
        stats_y = sem("stats_y")
        rstd_y_step = sem("rstd_y_step")
        rstd_y = sem("rstd_y")
        bn_x_done = sem("bn_x_done")
        stats_x = sem("stats_x")
        rstd_x_step = sem("rstd_x_step")
        rstd_x = sem("rstd_x")
        y_normed = sem("y_normed")
        yn_by_channel = sem("yn_by_channel")
        affine = sem("affine")
        z_done = sem("z_done")
        zhi_done = sem("zhi_done")
        zlo_done = sem("zlo_done")
        out_projected = sem("out_projected")
        residual = sem("residual")
        x1_done = sem("x1_done")
        row_hi = sem("row_hi")
        row_lo = sem("row_lo")
        x1_by_channel = sem("x1_by_channel")
        x1T_done = sem("x1T_done")
        routed = sem("routed")
        top_done = sem("top_done")
        top_kept = sem("top_kept")
        index_done = sem("index_done")
        chosen_done = sem("chosen_done")
        onehot_done = sem("onehot_done")
        mask_done = sem("mask_done")
        summed = sem("summed")
        counted = sem("counted")
        pos_done = sem("pos_done")
        pos_read = sem("pos_read")
        picked_done = sem("picked_done")
        slots_done = sem("slots_done")
        meta_done = sem("meta_done")
        token_next = sem("token_next")
        wf_scaled = sem("wf_scaled")
        wf_hi_done = sem("wf_hi_done")
        wf_lo_done = sem("wf_lo_done")

        slots_of = sb("slots_of", [P, E], F32)
        tiles_i = sb("tiles_i", [P, E], I32)
        tiles_of = sb("tiles_of", [P, E], F32)
        tiles_to = sb("tiles_to", [P, E], F32)
        skip_rows = sb("skip_rows", [P, E], F32)
        tail_f = sb("tail_f", [P, E], F32)
        tail_i = sb("tail_i", [P, E], I32)
        NT = NB * S
        at = TS * ROWF
        blank = gate[0][:, 0:at].rearrange("p (s w) -> p s w", s=TS)
        offset_f = gate[0][:, at:at + TILES]
        total = gate[0][:, at + TILES:at + TILES + NT]
        inv = gate[0][:, at + TILES + NT:at + TILES + 2 * NT]
        behind = gate[1][:, 0:TILES * E].rearrange("p (t e) -> p t e", e=E)
        prob = gate[1][:, TILES * E:TILES * E + 2 * NT].rearrange("p (t k) -> p t k", k=2)
        skipped = yn[:, 0:TILES * E].rearrange("p (t e) -> p t e", e=E)
        dif = x1T[:, 0:NT * E].rearrange("p (t e) -> p t e", e=E)
        total_slots = sem("total_slots")
        tail_done = sem("tail_done")
        table_step = sem("table_step")
        blanked = sem("blanked")
        dif_done = sem("dif_done")
        exp_done = sem("exp_done")

        N_PAR = 12

        def pipeline(eng, step):
            for i in range(4):
                step(i // 2, i % 2, True, i >= 1, i >= 2, i >= 3)
            with eng.Fori(2, NB // 2 - 1) as j:
                for u in range(2):
                    step(j, u, True, True, True, True)
            for u in range(2):
                step(NB // 2 - 1, u, True, True, True, True)
            step(NB // 2, 0, False, True, True, True)
            step(NB // 2, 1, False, False, True, True)
            step(NB // 2 + 1, 0, False, False, False, True)

        block = ctx.enter_context(nc.Block())

        @block.sync
        def _(sp):
            def keep_x1(b, u):
                sp.dma_start(x1[:, bass.ds(b * S * D, S * D)], x1_new[u][:, :]).then_inc(x1_kept[u], 16)

            def load(j, u):
                i = 2 * j + u
                wait(sp, x_hi, i - 1)
                wait(sp, x_lo, i - 1)
                sp.dma_start(xT32[u][:, :], io["xT"][i]).then_inc(xT_in[u], 16)
                if not (isinstance(i, int) and i == 0):
                    load_tokens(i - 1, 1 - u)

            def load_tokens(b, u):
                wait(sp, x1_done, b - 1)
                sp.dma_start(x_tok[u][:, :].rearrange("p (s d) -> p s d", s=S),
                             io["x_tok"][b]).then_inc(xtok_in[u], 16)
                if not (isinstance(b, int) and b < 2):
                    keep_x1(b - 2, u)

            load(0, 0)
            for dst, src in ((lam[:, :], io["lam"]), (keep_state[:, :], io["keep_state"]),
                             (ln_gb[:, :, :], io["ln_gb"]), (ident[:, :], io["ident"]),
                             (tri_ones[:, :, :], io["tri_ones"]), (iota_e[:, :], io["iota_e"]),
                             (region_base[:, :], io["region_base"]), (token0[:, :], io["token0"]),
                             (gate_w[:, :, :], io["gate_w"]), (tile_iota[:, :], io["tile_iota"]),
                             (keep["ident16"][:, :], io["ident16"]), (keep["b1"][:, :], io["b1"])):
                sp.dma_start(dst, src).then_inc(par_in, 16)
            for i in range(1, 4):
                load(i // 2, i % 2)
            with sp.Fori(2, NB // 2) as j:
                for u in range(2):
                    load(j, u)
            load_tokens(NB - 1, 1)
            for u in range(2):
                sp.wait_ge(x1_done, NB - 1 + u)
                keep_x1(NB - 2 + u, u)
            sp.wait_ge(tail_done, 1)
            for e in range(E):
                first = sp.value_load(tail_i[0:1, e:e + 1], min_val=0, max_val=E * REGION - TILE)
                sp.dma_start(region[bass.ds(first, TILE), :].rearrange("(s p) w -> p s w", p=P),
                             blank.bitcast(F16)).then_inc(blanked, 16)
            sp.dma_start(region[E * REGION:E * REGION + TILE, :].rearrange("(s p) w -> p s w", p=P),
                         blank.bitcast(F16)).then_inc(blanked, 16)
            for u in range(2):
                sp.wait_ge(x1_kept[u], 16 * NB // 2)
            sp.wait_ge(blanked, 16 * (E + 1))

        @block.tensor
        def _(pe):
            pe.wait_ge(wa_lo_done, 2)

            def project(c, parts=(0, 1, 2)):
                for n in parts:
                    w = (W_V, W_Q, W_G)[n]
                    dst = vqg[c][:, n * BLK:(n + 1) * BLK]
                    m = 0
                    for k in range(DC):
                        for a, b in ((wa_hi, xT_hi), (wa_lo, xT_hi), (wa_hi, xT_lo)):
                            last = nc.tensor.matmul(dst, a[:, w, k, c * P:(c + 1) * P], b[:, k, :],
                                                    start=(m == 0), stop=(m == 3 * DC - 1))
                            m += 1
                if 2 in parts:
                    last.then_inc(projected, 1)

            def enter(i):
                wait(pe, x_hi, i + 1)
                wait(pe, x_lo, i + 1)
                wait(pe, y_done, 2 * i - 1)
                project(1, (0,))

            enter(0)
            project(1, (1,))
            pe.wait_ge(par_in, 16 * N_PAR)
            pe.wait_ge(set_done, 1)

            def step(j, u, now, prev, prev2, prev3):
                i = 2 * j + u
                more = now and not (isinstance(i, int) and i == NB - 1)
                if now:
                    project(1, (2,))
                if prev3:
                    wait(pe, mask_done, i - 2)
                    wait(pe, counted, i - 3)
                    for s in range(S):
                        dst = ps_pos[:, s * E:(s + 1) * E]
                        nc.tensor.matmul(dst, tri_ones[:, 0, :], mask[:, s, :], start=True, stop=False)
                        for before in range(s):
                            nc.tensor.matmul(dst, tri_ones[:, 1, :], mask[:, before, :], start=False, stop=False)
                        last = nc.tensor.matmul(dst, tri_ones[:, 1, :], count_acc[:, :], start=False, stop=True)
                    last.then_inc(pos_done, 1)
                if prev:
                    wait(pe, y_normed, i)
                    wait(pe, residual, i - 1)
                    for c in range(DC):
                        for s in range(S):
                            last = nc.tensor.transpose(
                                ps_t[:, c * BLK + s * P:c * BLK + (s + 1) * P],
                                yn[:, s * D + c * P:s * D + (c + 1) * P], ident[:, :])
                    last.then_inc(yn_by_channel, 1)
                if now:
                    if prev3:
                        wait(pe, pos_read, i - 2)
                    project(0)
                if prev:
                    wait(pe, zlo_done, 2 * i - 1)
                    for s in range(S):
                        m = 0
                        for c in range(DC):
                            for a, b in ((z_hi, wa_hi), (z_hi, wa_lo), (z_lo, wa_hi)):
                                if s == 0 and c == 1 and m == 3:
                                    wait(pe, zhi_done, 2 * i)
                                if s == 0 and c == 1 and a is z_lo:
                                    wait(pe, zlo_done, 2 * i)
                                last = nc.tensor.matmul(ps_t[:, s * D:(s + 1) * D], a[:, c, s * P:(s + 1) * P],
                                                        b[:, W_O, c, :], start=(m == 0), stop=(m == 3 * DC - 1))
                                m += 1
                    last.then_inc(out_projected, 1)
                if now:
                    wait(pe, y_done, 2 * i + 2)
                    for s in range(S):
                        for c in range(DC):
                            last = nc.tensor.transpose(yT[:, s * D + c * P:s * D + (c + 1) * P],
                                                       y[:, c, s * P:(s + 1) * P], ident[:, :])
                    last.then_inc(y_by_token, 1)
                if more:
                    enter(i + 1)
                if prev2:
                    wait(pe, x1_done, i - 1)
                    if prev:
                        wait(pe, residual, i)
                    for c in range(DC):
                        for s in range(S):
                            last = nc.tensor.transpose(
                                ps_t[:, c * BLK + s * P:c * BLK + (s + 1) * P],
                                x1_new[u][:, s * D + c * P:s * D + (c + 1) * P], ident[:, :])
                    last.then_inc(x1_by_channel, 1)
                if more:
                    project(1, (1,))
                if prev2:
                    wait(pe, x1T_done, i - 1)
                    if not now:
                        wait(pe, pos_read, i - 2)
                    for s in range(S):
                        for c in range(DC):
                            last = nc.tensor.matmul(ps_logits[:, s * E:(s + 1) * E],
                                                    x1T[:, c * BLK + s * P:c * BLK + (s + 1) * P],
                                                    gate_w[:, c, :], start=(c == 0), stop=(c == DC - 1))
                    last.then_inc(routed, 1)

            pipeline(pe, step)
            pe.wait_ge(counted, NB)
            nc.tensor.matmul(ps_n, tri_ones[:, 1, :], count_acc[:, :], start=True,
                             stop=True).then_inc(total_slots, 1)

        @block.vector
        def _(dve):
            v = nc.vector
            v.memset(carry[:, :], 0.0)
            v.memset(count_acc[:, :], 0.0)
            v.memset(half_pow[:, :], -0.5)
            v.memset(eps[:, :], LN_EPS)
            v.memset(minus_one[:, :], -1.0)
            v.memset(blk[:, :], float(BLK))
            v.memset(ones_e[:, :], 1.0)
            for u in range(2):
                last = v.memset(row[u][:, :, :], 0.0)
            last.then_inc(set_done, 1)
            for h in range(2):
                dve.wait_ge(wa_hi_done, h + 1)
                v.scalar_tensor_tensor(out=wa_lo[:, :, h, :], in0=wa32[h], scalar=WSCALE,
                                       in1=wa_hi[:, :, h, :], op0=ALU.mult,
                                       op1=ALU.subtract).then_inc(wa_lo_done, 1)

            dve.wait_ge(par_in, 16 * N_PAR)
            dve.wait_ge(set_done, 1)
            v.tensor_scalar(ln_gb[:, :, :], ln_gb[:, :, :], 0.5 / WSCALE, None, ALU.mult).then_inc(set_done, 1)
            def split_x(b, u):
                wait(dve, x_hi, b + 1)
                wait(dve, projected, 2 * b)
                v.tensor_tensor(xT_lo[:, :, :], xT32[u][:, :].rearrange("p (c t) -> p c t", c=DC),
                                xT_hi[:, :, :], ALU.subtract).then_inc(x_lo, 1)

            def retain(i, u, c):
                n = 1 - c
                wait(dve, projected, 2 * i + n + 1)
                wait(dve, carried, 2 * i + n - 1)
                if n == 0:
                    wait(dve, y_by_token, i)
                v.tensor_tensor_scan(y[:, c, :], lam[:, c:c + 1].broadcast_to([P, BLK]),
                                     vqg[c][:, 0:BLK], carry[:, c:c + 1], ALU.mult,
                                     ALU.add).then_inc(scanned, 1)
                wait(dve, tanh_done, 2 * i + n + 1)
                g = gate[u][:, c * BLK:(c + 1) * BLK]
                v.scalar_tensor_tensor(out=g, in0=g, scalar=1.0, in1=vqg[c][:, 2 * BLK:3 * BLK],
                                       op0=ALU.add, op1=ALU.mult).then_inc(gated, 1)
                wait(dve, scanned, 2 * i + n + 1)
                v.tensor_scalar(carry[:, c:c + 1], y[:, c, BLK - 1:BLK], keep_state[:, bass.ds(i + 1, 1)], None,
                                ALU.mult).then_inc(carried, 1)
                wait(dve, carried, 2 * i + n + 1)
                v.scalar_tensor_tensor(out=y[:, c, :], in0=vqg[c][:, BLK:2 * BLK],
                                       scalar=1.0 / (WSCALE * WSCALE), in1=y[:, c, :],
                                       op0=ALU.mult, op1=ALU.mult).then_inc(y_done, 1)

            split_x(0, 0)

            def step(j, u, now, prev, prev2, prev3):
                i = 2 * j + u
                b = i - 2
                if prev3:
                    wait(dve, pos_done, b)
                    v.tensor_tensor(position[:, :, :], ps_pos.rearrange("p (s e) -> p s e", s=S),
                                    region_base[:, :].unsqueeze(1).broadcast_to([P, S, E]),
                                    ALU.add).then_inc(pos_read, 1)
                if now:
                    retain(i, u, 1)
                if prev:
                    wait(dve, gated, 2 * i)
                    for c in range(DC):
                        half = slice(c * BLK, (c + 1) * BLK)
                        wait(dve, affine, 2 * i - 1 + c)
                        v.tensor_tensor(yn[:, half], yn[:, half], gate[1 - u][:, half], ALU.mult).then_inc(z_done, 1)
                if prev3:
                    wait(dve, summed, b)
                    v.tensor_tensor(count_acc[:, :], count_acc[:, :], block_sum[:, :], ALU.add).then_inc(counted, 1)
                    wait(dve, pos_read, b)
                    v.tensor_tensor(picked[:, :, :, :], onehot[:, :, :, :],
                                    position[:, :, :].unsqueeze(1).broadcast_to([P, 2, S, E]),
                                    ALU.mult).then_inc(picked_done, 1)
                    wait(dve, picked_done, b)
                    with nc.allow_low_precision("row numbers are whole and below 2^24"):
                        v.tensor_reduce(slot[1 - u][:, :, :], picked[:, :, :, :], AX_X, ALU.add).then_inc(slots_done, 1)
                if prev:
                    wait(dve, out_projected, i - 1)
                    for c in range(DC):
                        wait(dve, zhi_done, 2 * i - 1 + c)
                        v.tensor_tensor(z_lo[:, c, :], yn[:, c * BLK:(c + 1) * BLK], z_hi[:, c, :],
                                        ALU.subtract).then_inc(zlo_done, 1)
                if now:
                    retain(i, u, 0)
                    if not (isinstance(i, int) and i == NB - 1):
                        split_x(i + 1, 1 - u)
                if prev:
                    wait(dve, out_projected, i)
                    wait(dve, xtok_in[1 - u], 16 * (j + u))
                    t = x_tok[1 - u]
                    v.scalar_tensor_tensor(out=t[:, :], in0=ps_t[:, :], scalar=1.0 / WSCALE, in1=t[:, :],
                                           op0=ALU.mult, op1=ALU.add).then_inc(residual, 1)
                if now:
                    wait(dve, rstd_y, i)
                    wait(dve, y_by_token, i + 1)
                    for s in range(S):
                        last = v.bn_stats(bn_y[:, s, :], yT[:, s * D:(s + 1) * D])
                    last.then_inc(bn_y_done, 1)
                    wait(dve, bn_y_done, i + 1, beside=(set_done, 1))
                    for s in range(S):
                        last = v.bn_aggr(mv_y[:, s, :], bn_y[:, s, :])
                    last.then_inc(stats_y, 1)
                if prev:
                    wait(dve, rstd_x, i - 1)
                    wait(dve, residual, i)
                    for s in range(S):
                        last = v.bn_stats(bn_x[:, s, :], t[:, s * D:(s + 1) * D])
                    last.then_inc(bn_x_done, 1)
                    wait(dve, bn_x_done, i, beside=(set_done, 1))
                    for s in range(S):
                        last = v.bn_aggr(mv_x[:, s, :], bn_x[:, s, :])
                    last.then_inc(stats_x, 1)
                if prev2:
                    rowh = row[u][:, :, :].bitcast(F16)

                    def row_low(s):
                        return v.tensor_tensor(rowh[:, s, D:2 * D], x1_new[u][:, s * D:(s + 1) * D],
                                               rowh[:, s, 0:D], ALU.subtract)

                    wait(dve, routed, b + 1)
                    wait(dve, top_kept, b)
                    wait(dve, row_hi, b + 1)
                    row_low(0)
                    for s in range(S):
                        last = v.max(m8_new[:, s, :], ps_logits[:, s * E:(s + 1) * E])
                    last.then_inc(top_done, 1)
                    row_low(1)
                    wait(dve, top_done, b + 1, beside=(set_done, 1))
                    for s in range(S):
                        last = v.max_index(i8[:, s, :], m8_new[:, s, :], ps_logits[:, s * E:(s + 1) * E])
                    last.then_inc(index_done, 1)
                    row_low(2)
                    wait(dve, index_done, b + 1)
                    wait(dve, meta_done, b)
                    v.tensor_copy(chosen[:, :, :], i8[:, :, 0:2].rearrange("p s k -> p k s")
                                  ).then_inc(chosen_done, 1)
                    row_low(3).then_inc(row_lo, 1)
                    wait(dve, chosen_done, b + 1)
                    v.tensor_tensor(onehot[:, :, :, :],
                                    iota_e[:, :].unsqueeze(1).unsqueeze(1).broadcast_to([P, 2, S, E]),
                                    chosen[:, :, :].unsqueeze(3).broadcast_to([P, 2, S, E]),
                                    ALU.is_equal).then_inc(onehot_done, 1)
                    wait(dve, onehot_done, b + 1)
                    v.tensor_tensor(mask[:, :, :], onehot[:, 0, :, :], onehot[:, 1, :, :],
                                    ALU.add).then_inc(mask_done, 1)
                    wait(dve, mask_done, b + 1)
                    v.tensor_reduce(block_sum[:, :], mask[:, :, :].rearrange("p s e -> p e s"), AX_X,
                                    ALU.add).then_inc(summed, 1)

            pipeline(dve, step)

            steps = [0]

            def link(ins):
                steps[0] += 1
                ins.then_inc(table_step, 1)
                dve.wait_ge(table_step, steps[0])

            link(v.memset(blank, 0.0))
            v.memset(blank[:, :, META], NO_TOKEN)
            v.memset(blank[:, :, META + 1], -1.0)
            dve.wait_ge(total_slots, 1)
            link(v.tensor_copy(slots_of[:, :], ps_n))
            v.tensor_scalar(tiles_i[:, :], slots_of[:, :], float(TILE - 1), None, ALU.add)
            link(v.tensor_tensor(tail_f[:, :], region_base[:, :], slots_of[:, :], ALU.add))
            v.tensor_copy(tail_i[:, :], tail_f[:, :]).then_inc(tail_done, 1)
            link(v.tensor_scalar(tiles_i[:, :], tiles_i[:, :], TILE.bit_length() - 1, None, ALU.arith_shift_right))
            link(v.tensor_copy(tiles_of[:, :], tiles_i[:, :]))
            v.tensor_scalar(skip_rows[:, :], tiles_of[:, :], -float(TILE), float(REGION), ALU.mult, ALU.add)
            link(v.tensor_tensor_scan(tiles_to[:, :], ones_e[:, :], tiles_of[:, :], 0.0, ALU.mult, ALU.add))
            v.tensor_scalar(offset_f, tile_iota[:, :], float(TILE), None, ALU.mult)
            link(v.tensor_tensor(behind, tile_iota[:, :].unsqueeze(2).broadcast_to([P, TILES, E]),
                                 tiles_to[:, :].unsqueeze(1).broadcast_to([P, TILES, E]), ALU.is_ge))
            v.tensor_reduce(expert_f[:, :], behind, AX_X, ALU.add)
            link(v.tensor_tensor(skipped, behind, skip_rows[:, :].unsqueeze(1).broadcast_to([P, TILES, E]), ALU.mult))
            link(v.tensor_reduce(behind[:, :, 0], skipped, AX_X, ALU.add))
            v.tensor_scalar(expert_f[:, :], expert_f[:, :], float(E - 1), None, ALU.min)
            link(v.tensor_tensor(offset_f, offset_f, behind[:, :, 0], ALU.add))
            v.tensor_scalar(offset_i[:, :], offset_f, float(E * REGION), None, ALU.min)
            link(v.tensor_copy(expert_i[:, :], expert_f[:, :]))

            dve.wait_ge(top_kept, NB)
            m8v = m8[:, :].rearrange("p (t e) -> p t e", e=E)
            v.tensor_tensor(dif, m8v, m8v[:, :, 0:1].broadcast_to([P, NT, E]), ALU.subtract).then_inc(dif_done, 1)
            dve.wait_ge(exp_done, 1)
            link(v.tensor_reduce(total, dif, AX_X, ALU.add))
            link(v.reciprocal(inv, total))
            link(v.tensor_tensor(prob, dif[:, :, 0:2], inv.unsqueeze(2).broadcast_to([P, NT, 2]), ALU.mult))
            link(v.tensor_tensor(total, prob[:, :, 0], prob[:, :, 1], ALU.add))
            link(v.tensor_scalar(total, total, 1e-8, 2.0, ALU.add, ALU.mult))
            link(v.reciprocal(inv, total))
            link(v.tensor_tensor(cw[:, :].rearrange("p (t k) -> p t k", k=2), prob,
                                 inv.unsqueeze(2).broadcast_to([P, NT, 2]), ALU.mult))

        @block.scalar
        def _(act):
            a = nc.scalar
            for h in range(2):
                act.dma_start(wa32[h], io["wa"][h]).then_inc(wa_in[h], 16)
            for h in range(2):
                act.wait_ge(wa_in[h], 16)
                a.activation(wa_hi[:, :, h, :], wa32[h], ACT.Copy, scale=WSCALE).then_inc(wa_hi_done, 1)

            def split_x(b, u, loads):
                wait(act, xT_in[u], 16 * loads)
                wait(act, projected, 2 * b)
                a.activation(xT_hi[:, :, :], xT32[u][:, :].rearrange("p (c t) -> p c t", c=DC),
                             ACT.Copy).then_inc(x_hi, 1)

            split_x(0, 0, 1)

            def step(j, u, now, prev, prev2, prev3):
                i = 2 * j + u
                if now:
                    wait(act, projected, 2 * i + 1)
                    wait(act, z_done, 2 * i - 2)
                    a.activation(gate[u][:, BLK:2 * BLK], ps_b[:, 2 * BLK:3 * BLK], ACT.Tanh,
                                 scale=0.5 / WSCALE).then_inc(tanh_done, 1)
                if prev:
                    wait(act, yn_by_channel, i)
                    wait(act, set_done, 2)
                    for c in range(DC):
                        a.activation(yn[:, c * BLK:(c + 1) * BLK], ps_t[:, c * BLK:(c + 1) * BLK], ACT.Identity,
                                     scale=ln_gb[:, 0, c:c + 1], bias=ln_gb[:, 1, c:c + 1]).then_inc(affine, 1)
                    wait(act, wf_in, 16 * i)
                    a.activation(wf32[:, :], wf32[:, :], ACT.Copy, scale=WSCALE).then_inc(wf_scaled, 1)
                    wait(act, out_projected, i - 1)
                    for c in range(DC):
                        wait(act, z_done, 2 * i - 1 + c)
                        a.activation(z_hi[:, c, :], yn[:, c * BLK:(c + 1) * BLK], ACT.Copy).then_inc(zhi_done, 1)
                    wait(act, wf_scaled, i)
                    a.activation(wf16[:, bass.ds((i - 1) * 2 * DC * HID, DC * HID)], wf32[:, :],
                                 ACT.Copy).then_inc(wf_hi_done, 1)
                if now:
                    wait(act, projected, 2 * i + 2)
                    a.activation(gate[u][:, 0:BLK], ps_a[:, 2 * BLK:3 * BLK], ACT.Tanh,
                                 scale=0.5 / WSCALE).then_inc(tanh_done, 1)
                    if not (isinstance(i, int) and i == NB - 1):
                        split_x(i + 1, 1 - u, j + u + 1)
                if prev2:
                    wait(act, rstd_x, i - 1)
                    wait(act, x1_by_channel, i - 3)
                    wait(act, row_lo, i - 3)
                    wait(act, x1_kept[u], 16 * (j - 1))
                    for s in range(S):
                        last = a.activation(x1_new[u][:, s * D:(s + 1) * D], x_tok[u][:, s * D:(s + 1) * D],
                                            ACT.Identity, scale=rs_x[:, 1, s:s + 1], bias=rs_x[:, 2, s:s + 1])
                    last.then_inc(x1_done, 1)
                    wait(act, x1_done, i - 1)
                    wait(act, scattered[u], 128 * (j - 1))
                    wait(act, set_done, 1)
                    a.activation(row[u][:, :, :].bitcast(F16)[:, :, 0:D],
                                 x1_new[u][:, :].rearrange("p (s d) -> p s d", s=S),
                                 ACT.Copy).then_inc(row_hi, 1)
                if prev2:
                    wait(act, x1_by_channel, i - 1)
                    wait(act, routed, i - 2)
                    a.activation(x1T[:, :], ps_t[:, :], ACT.Copy).then_inc(x1T_done, 1)
                if now:
                    wait(act, wf_lo_done, i)
                    act.dma_start(wf32[:, :], io["wf"][i]).then_inc(wf_in, 16)
                    wait(act, rstd_y, i + 1)
                    wait(act, zlo_done, 2 * i)
                    for s in range(S):
                        last = a.activation(yn[:, s * D:(s + 1) * D], yT[:, s * D:(s + 1) * D], ACT.Identity,
                                            scale=rs_y[:, 1, s:s + 1], bias=rs_y[:, 2, s:s + 1])
                    last.then_inc(y_normed, 1)

            pipeline(act, step)
            act.wait_ge(dif_done, 1)
            a.activation(dif, dif, ACT.Exp).then_inc(exp_done, 1)

        @block.gpsimd
        def _(pool):
            g = nc.gpsimd
            pool.wait_ge(par_in, 16 * N_PAR)
            pool.wait_ge(set_done, 1)
            zeros_set = (set_done, 1)

            g.tensor_copy(token[:, :], token0[:, :]).then_inc(token_next, 1)

            def rstd(mv, rs, stepped, done, n):
                g.tensor_tensor(rs[:, 2, :], mv[:, :, 0], minus_one[:, :], ALU.mult)
                g.tensor_tensor(rs[:, 0, :], mv[:, :, 1], eps[:, :], ALU.add).then_inc(stepped, 1)
                wait(pool, stepped, 2 * n + 1)
                g.tensor_tensor(rs[:, 1, :], rs[:, 0, :], half_pow[:, :], ALU.pow).then_inc(stepped, 1)
                wait(pool, stepped, 2 * n + 2)
                g.tensor_tensor(rs[:, 2, :], rs[:, 2, :], rs[:, 1, :], ALU.mult).then_inc(done, 1)

            def scatter(u, k):
                for s in range(S):
                    g.indirect_dma_start(region, bass.IndirectOffsetOnAxis(slot[u][:, k, s:s + 1], 0),
                                         row[u][:, s, :].bitcast(F16), None).then_inc(scattered[u], 16)

            def step(j, u, now, prev, prev2, prev3):
                i = 2 * j + u
                b = i - 2
                if prev3:
                    wait(pool, meta_done, b)
                    g.tensor_tensor(token[:, :], token[:, :], blk[:, :], ALU.add).then_inc(token_next, 1)
                    wait(pool, slots_done, b, beside=zeros_set)
                    wait(pool, row_lo, b, beside=zeros_set)
                    scatter(1 - u, 0)
                if prev:
                    wait(pool, wf_hi_done, i)
                    base = (i - 1) * 2 * DC * HID
                    g.tensor_tensor(wf16[:, bass.ds(base + DC * HID, DC * HID)], wf32[:, :],
                                    wf16[:, bass.ds(base, DC * HID)], ALU.subtract).then_inc(wf_lo_done, 1)
                if now:
                    wait(pool, stats_y, i + 1)
                    wait(pool, y_normed, i)
                    rstd(mv_y, rs_y, rstd_y_step, rstd_y, i)
                if prev3:
                    scatter(1 - u, 1)
                if prev:
                    wait(pool, stats_x, i)
                    wait(pool, x1_done, i - 1)
                    rstd(mv_x, rs_x, rstd_x_step, rstd_x, i - 1)
                if prev2:
                    wait(pool, chosen_done, b + 1, beside=zeros_set)
                    g.tensor_copy(m8[:, bass.ds(b * S * E, S * E)],
                                  m8_new[:, :, :].rearrange("p s e -> p (s e)")).then_inc(top_kept, 1)
                    wait(pool, row_hi, b + 1, beside=zeros_set)
                    wait(pool, token_next, b + 1, beside=zeros_set)
                    g.tensor_copy(row[u][:, :, META], token[:, :])
                    g.tensor_copy(row[u][:, :, META + 1], chosen[:, 1, :]).then_inc(meta_done, 1)

            pipeline(pool, step)
            for u in range(2):
                pool.wait_ge(scattered[u], 128 * NB // 2)


def build_experts(nc, io, keep):
    wf16, expert_f, expert_i, offset_i, ident16, b1 = (
        keep[n] for n in ("wf16", "expert_f", "expert_i", "offset_i", "ident16", "b1"))
    region, outputs = io["region"], io["outputs"]
    WE = 4 * DC * HID
    with ExitStack() as ctx:
        def sb(name, shape, dt):
            return ctx.enter_context(nc.sbuf_tensor(name, shape, dt))

        def psum(name, shape, dt):
            return ctx.enter_context(nc.psum_tensor(name, shape, dt))

        def sem(name):
            return ctx.enter_context(nc.semaphore(name))

        b2 = sb("b2", [P, E * D], F32)
        rows = [sb(f"rows_{u}", [P, TS, ROWF], F32) for u in range(2)]
        xT = [sb(f"xT_{u}", [P, 2 * DC * TILE], F16) for u in range(2)]
        h = [sb(f"h_{u}", [P, HC * TILE], F32) for u in range(2)]
        h_hi = [sb(f"h_hi_{u}", [P, HC * TILE], F16) for u in range(2)]
        h_lo = [sb(f"h_lo_{u}", [P, HC * TILE], F16) for u in range(2)]
        y_out = [sb(f"y_out_{u}", [P, TS * D], F32) for u in range(2)]
        is_second = [sb(f"is_second_{u}", [P, TS], F32) for u in range(2)]
        token = [sb(f"token_of_{u}", [P, TS], F32) for u in range(2)]
        dest_f = sb("dest_f", [P, TS], F32)
        dest = [sb(f"dest_{u}", [P, TS], U32) for u in range(2)]

        ps_x = psum("ps_x", [P, 2 * DC * TILE], F16)
        ps_h = [psum(f"ps_h_{u}", [P, HC * TILE], F32) for u in range(2)]
        ps_y = [psum(f"ps_y_{u}", [P, TS * D], F32) for u in range(2)]

        b2_in = sem("b2_in")
        rows_in = [sem("rows_in_0"), sem("rows_in_1")]
        scattered = [sem("y_scattered_0"), sem("y_scattered_1")]
        x_transposed = sem("x_transposed")
        x_copied = sem("x_copied")
        hidden = sem("hidden")
        relu_done = sem("relu_done")
        h_hi_done = sem("h_hi_done")
        h_lo_done = sem("h_lo_done")
        projected = sem("y_projected")
        second_done = sem("second_done")
        dest_f_done = sem("dest_f_done")
        dest_done = sem("dest_done")
        y_ready = sem("y_ready")

        def pipeline(eng, step):
            for t in range(4):
                step(t // 2, t % 2, True, True)
            with eng.Fori(2, TILES // 2) as j:
                for u in range(2):
                    step(j, u, True, True)
            step(TILES // 2, 0, True, False)
            step(TILES // 2, 1, False, False)

        assert TILES % 2 == 1
        block = ctx.enter_context(nc.Block())

        @block.sync
        def _(sp):
            def load(j, u):
                t = 2 * j + u
                wait(sp, x_transposed, t - 1)
                wait(sp, second_done, t - 1)
                first = sp.value_load(offset_i[0:1, bass.ds(t, 1)], min_val=0, max_val=E * REGION)
                sp.dma_start(rows[u][:, :, :].bitcast(F16),
                             region[bass.ds(first, TILE), :].rearrange("(s p) w -> p s w", p=P)
                             ).then_inc(rows_in[u], 16)

            for t in range(4):
                load(t // 2, t % 2)
            with sp.Fori(2, TILES // 2) as j:
                for u in range(2):
                    load(j, u)
            load(TILES // 2, 0)

        @block.tensor
        def _(pe):
            def transpose_rows(t, u, loads):
                wait(pe, rows_in[u], 16 * loads)
                wait(pe, x_copied, t)
                src = rows[u][:, :, :].bitcast(F16)
                for half in range(2):
                    for k in range(DC):
                        for s in range(TS):
                            at = (half * DC + k) * TILE + s * P
                            last = nc.tensor.transpose(ps_x[:, at:at + P],
                                                       src[:, s, half * D + k * P:half * D + (k + 1) * P],
                                                       ident16[:, :])
                last.then_inc(x_transposed, 1)

            transpose_rows(0, 0, 1)

            def step(j, u, now, after):
                t = 2 * j + u
                if now:
                    e = pe.value_load(expert_i[0:1, bass.ds(t, 1)], min_val=0, max_val=E - 1)
                    wait(pe, x_copied, t + 1)
                    wait(pe, relu_done, 2 * (t - 1))
                    for c in range(HC):
                        m = 0
                        for k in range(DC):
                            for wl, xl in ((0, 0), (1, 0), (0, 1)):
                                last = nc.tensor.matmul(
                                    ps_h[u][:, c * TILE:(c + 1) * TILE],
                                    wf16[:, bass.ds(e * WE + (wl * DC + k) * HID + c * P, P)],
                                    xT[u][:, (xl * DC + k) * TILE:(xl * DC + k + 1) * TILE],
                                    start=(m == 0), stop=(m == 3 * DC - 1))
                                m += 1
                        if c % 2:
                            last.then_inc(hidden, 1)
                if after:
                    transpose_rows(t + 1, 1 - u, j + u + 1)
                if not (isinstance(t, int) and t == 0):
                    e = pe.value_load(expert_i[0:1, bass.ds(t - 1, 1)], min_val=0, max_val=E - 1)
                    wait(pe, h_lo_done, t)
                    wait(pe, y_ready, t - 2)
                    for s in range(TS):
                        m = 0
                        for k in range(HC):
                            for hl, wl in ((h_hi, 0), (h_lo, 0), (h_hi, 1)):
                                last = nc.tensor.matmul(
                                    ps_y[1 - u][:, s * D:(s + 1) * D],
                                    hl[1 - u][:, k * TILE + s * P:k * TILE + (s + 1) * P],
                                    wf16[:, bass.ds(e * WE + 2 * DC * HID + (wl * HC + k) * D, D)],
                                    start=(m == 0), stop=(m == 3 * HC - 1))
                                m += 1
                    last.then_inc(projected, 1)

            pipeline(pe, step)

        @block.vector
        def _(dve):
            v = nc.vector
            def take_x(t, u):
                wait(dve, x_transposed, t + 1)
                wait(dve, hidden, 2 * (t - 1))
                v.tensor_copy(xT[u][:, :], ps_x[:, :]).then_inc(x_copied, 1)

            take_x(0, 0)
            def step(j, u, now, after):
                t = 2 * j + u
                if now:
                    wait(dve, rows_in[u], 16 * (j + 1))
                    wait(dve, dest_f_done, t - 1)
                    v.tensor_copy(token[u][:, :], rows[u][:, :, META])
                    v.tensor_scalar(is_second[u][:, :], rows[u][:, :, META + 1], expert_f[:, bass.ds(t, 1)],
                                    float(TOKENS), ALU.is_equal, ALU.mult).then_inc(second_done, 1)
                if after:
                    take_x(t + 1, 1 - u)
                if now:
                    wait(dve, h_hi_done, t + 1)
                    wait(dve, projected, t - 1)
                    v.tensor_tensor(h_lo[u][:, :], h[u][:, :], h_hi[u][:, :], ALU.subtract).then_inc(h_lo_done, 1)
                if not (isinstance(t, int) and t == 0):
                    if isinstance(t, int) and t == 1:
                        dve.wait_ge(b2_in, 16)
                    e = dve.value_load(expert_i[0:1, bass.ds(t - 1, 1)], min_val=0, max_val=E - 1)
                    wait(dve, projected, t)
                    if not (isinstance(t, int) and t < 3):
                        wait(dve, scattered[1 - u], 32 * (j + u - 1))
                    v.scalar_tensor_tensor(out=y_out[1 - u][:, :].rearrange("p (s d) -> p s d", s=TS),
                                           in0=ps_y[1 - u][:, :].rearrange("p (s d) -> p s d", s=TS),
                                           scalar=1.0 / WSCALE,
                                           in1=b2[:, bass.ds(e * D, D)].unsqueeze(1).broadcast_to([P, TS, D]),
                                           op0=ALU.mult, op1=ALU.add).then_inc(y_ready, 1)

            pipeline(dve, step)

        @block.scalar
        def _(act):
            a = nc.scalar
            act.dma_start(b2[:, :], io["b2"].partition_broadcast(P)).then_inc(b2_in, 16)

            def step(j, u, now, after):
                t = 2 * j + u
                if not now:
                    return
                e = act.value_load(expert_i[0:1, bass.ds(t, 1)], min_val=0, max_val=E - 1)
                wait(act, h_lo_done, t - 1)
                for c in range(HC):
                    if c % 2 == 0:
                        wait(act, hidden, 2 * t + c // 2 + 1)
                    last = a.activation(h[u][:, c * TILE:(c + 1) * TILE], ps_h[u][:, c * TILE:(c + 1) * TILE],
                                        ACT.Relu, scale=1.0 / WSCALE, bias=b1[:, bass.ds(e * HC + c, 1)])
                    if c % 2:
                        last.then_inc(relu_done, 1)
                wait(act, relu_done, 2 * t + 2)
                wait(act, projected, t - 1)
                a.activation(h_hi[u][:, :], h[u][:, :], ACT.Copy).then_inc(h_hi_done, 1)

            pipeline(act, step)

        @block.gpsimd
        def _(pool):
            pool.wait_ge(b2_in, 16)
            b2_set = (b2_in, 16)

            def step(j, u, now, after):
                t = 2 * j + u
                if isinstance(t, int) and t == 0:
                    return
                wait(pool, second_done, t)
                if not (isinstance(t, int) and t < 3):
                    wait(pool, scattered[1 - u], 32 * (j + u - 1))
                nc.gpsimd.tensor_tensor(dest_f[:, :], is_second[1 - u][:, :], token[1 - u][:, :],
                                        ALU.add).then_inc(dest_f_done, 1)
                wait(pool, dest_f_done, t, beside=b2_set)
                nc.gpsimd.tensor_copy(dest[1 - u][:, :], dest_f[:, :]).then_inc(dest_done, 1)
                wait(pool, dest_done, t, beside=b2_set)
                wait(pool, y_ready, t, beside=b2_set)
                for s in range(TS):
                    nc.gpsimd.indirect_dma_start(outputs, bass.IndirectOffsetOnAxis(dest[1 - u][:, s:s + 1], 0),
                                                 y_out[1 - u][:, s * D:(s + 1) * D], None,
                                                 bounds_check=2 * TOKENS - 1,
                                                 oob_is_err=False).then_inc(scattered[1 - u], 16)

            pipeline(pool, step)
            pool.wait_ge(scattered[0], 32 * (TILES // 2 + 1))
            pool.wait_ge(scattered[1], 32 * (TILES // 2))


def build_combine(nc, io, keep):
    x1, cw = keep["x1"], keep["cw"]
    y2 = io["outputs"].rearrange("(k b s p) d -> k b p s d", k=2, b=NB, p=P)
    out = io["out"].rearrange("(b s p) d -> b p s d", b=NB, p=P)
    BUFS = 4
    with ExitStack() as ctx:
        def sb(name, shape, dt):
            return ctx.enter_context(nc.sbuf_tensor(name, shape, dt))

        def sem(name):
            return ctx.enter_context(nc.semaphore(name))

        first = [sb(f"first_{u}", [P, S, D], F32) for u in range(BUFS)]
        second = [sb(f"second_{u}", [P, S, D], F32) for u in range(BUFS)]
        both = [sb(f"both_{u}", [P, S, D], F32) for u in range(BUFS)]
        half_pow = sb("half_pow_2", [P, S], F32)
        eps = sb("eps_2", [P, S], F32)
        minus_one = sb("minus_one_2", [P, S], F32)
        bn = [sb(f"bn_2_{u}", [P, S, 6], F32) for u in range(2)]
        mv = [sb(f"mv_2_{u}", [P, S, 2], F32) for u in range(2)]
        rs = [sb(f"rs_2_{u}", [P, 3, S], F32) for u in range(2)]
        first_in = [sem(f"first_in_{u}") for u in range(BUFS)]
        second_in = [sem(f"second_in_{u}") for u in range(BUFS)]
        stored = [sem(f"stored_{u}") for u in range(BUFS)]
        set_done = sem("set_done_2")
        added = sem("added")
        weighted = sem("weighted")
        summed = sem("summed_2")
        bn_done = sem("bn_done_2")
        stats = sem("stats_2")
        rstd_step = sem("rstd_step_2")
        rstd = sem("rstd_2")
        norm_done = sem("norm_done")

        def pipeline(eng, step):
            for u in range(BUFS):
                step(0, u, True, u >= 1, u >= 2)
            with eng.Fori(1, NB // BUFS) as j:
                for u in range(BUFS):
                    step(j, u, True, True, True)
            step(NB // BUFS, 0, False, True, True)
            step(NB // BUFS, 1, False, False, True)

        block = ctx.enter_context(nc.Block())

        @block.sync
        def _(sp):
            def step(j, u, now, prev, prev2):
                if now:
                    wait(sp, added, BUFS * (j - 1) + u + 1)
                    sp.dma_start(first[u][:, :, :], y2[0, j * BUFS + u]).then_inc(first_in[u], 16)
                    wait(sp, summed, BUFS * (j - 1) + u + 1)
                    sp.dma_start(second[u][:, :, :], y2[1, j * BUFS + u]).then_inc(second_in[u], 16)

            pipeline(sp, step)

        @block.vector
        def _(dve):
            v = nc.vector
            v.memset(eps[:, :], LN_EPS / 4)
            v.memset(minus_one[:, :], -1.0)
            v.memset(half_pow[:, :], -0.5).then_inc(set_done, 1)

            def step(j, u, now, prev, prev2):
                i = BUFS * j + u
                w = u % 2
                if now:
                    wait(dve, rstd, i - 2)
                    wait(dve, first_in[u], 16 * (j + 1))
                    wait(dve, stored[u], 16 * j)
                    for s in range(S):
                        last = v.scalar_tensor_tensor(out=both[u][:, s, :], in0=first[u][:, s, :],
                                                      scalar=cw[:, bass.ds((i * S + s) * 2, 1)],
                                                      in1=x1[:, bass.ds((i * S + s) * D, D)],
                                                      op0=ALU.mult, op1=ALU.add)
                    last.then_inc(added, 1)
                if prev:
                    if not now:
                        wait(dve, rstd, i - 2)
                    wait(dve, bn_done, i, beside=(set_done, 1))
                    for s in range(S):
                        last = v.bn_aggr(mv[1 - w][:, s, :], bn[1 - w][:, s, :])
                    last.then_inc(stats, 1)
                if now:
                    wait(dve, added, i + 1)
                    wait(dve, weighted, i + 1)
                    v.tensor_tensor(both[u][:, :, :], both[u][:, :, :], second[u][:, :, :],
                                    ALU.add).then_inc(summed, 1)
                    wait(dve, summed, i + 1)
                    for s in range(S):
                        last = v.bn_stats(bn[w][:, s, :], both[u][:, s, :])
                    last.then_inc(bn_done, 1)

            pipeline(dve, step)

        @block.gpsimd
        def _(pool):
            g = nc.gpsimd
            pool.wait_ge(set_done, 1)

            def step(j, u, now, prev, prev2):
                i = BUFS * j + u
                if prev:
                    w = (u + 1) % 2
                    wait(pool, stats, i)
                    wait(pool, norm_done, i - 2)
                    g.tensor_tensor(rs[w][:, 2, :], mv[w][:, :, 0], minus_one[:, :], ALU.mult)
                    g.tensor_tensor(rs[w][:, 0, :], mv[w][:, :, 1], eps[:, :], ALU.add).then_inc(rstd_step, 1)
                    wait(pool, rstd_step, 2 * i - 1)
                    g.tensor_tensor(rs[w][:, 1, :], rs[w][:, 0, :], half_pow[:, :], ALU.pow).then_inc(rstd_step, 1)
                    wait(pool, rstd_step, 2 * i)
                    g.tensor_tensor(rs[w][:, 2, :], rs[w][:, 2, :], rs[w][:, 1, :], ALU.mult).then_inc(rstd, 1)

            pipeline(pool, step)

        @block.scalar
        def _(act):
            a = nc.scalar

            def step(j, u, now, prev, prev2):
                i = BUFS * j + u
                if now:
                    wait(act, second_in[u], 16 * (j + 1))
                    for s in range(S):
                        last = a.activation(second[u][:, s, :], second[u][:, s, :], ACT.Copy,
                                            scale=cw[:, bass.ds((i * S + s) * 2 + 1, 1)])
                    last.then_inc(weighted, 1)
                if prev2:
                    w, u2 = u % 2, (u + 2) % BUFS
                    wait(act, rstd, i - 1)
                    for s in range(S):
                        last = a.activation(both[u2][:, s, :], both[u2][:, s, :], ACT.Identity,
                                            scale=rs[w][:, 1, s:s + 1], bias=rs[w][:, 2, s:s + 1])
                    last.then_inc(norm_done, 1)
                    wait(act, norm_done, i - 1)
                    act.dma_start(out[i - 2], both[u2][:, :, :]).then_inc(stored[u2], 16)

            pipeline(act, step)
            for u in range(BUFS):
                act.wait_ge(stored[u], 16 * NB // BUFS)


def build(nc, io):
    io["region"] = nc.dram_tensor("region", [E * REGION + TILE, ROW], F16, kind="Internal").ap()
    io["outputs"] = nc.dram_tensor("outputs", [2 * TOKENS, D], F32, kind="Internal").ap()
    with ExitStack() as ctx:
        keep = {
            "x1": ctx.enter_context(nc.sbuf_tensor("x1", [P, NB * S * D], F32)),
            "wf16": ctx.enter_context(nc.sbuf_tensor("wf16", [P, E * 4 * DC * HID], F16)),
            "m8": ctx.enter_context(nc.sbuf_tensor("m8", [P, NB * S * E], F32)),
            "expert_f": ctx.enter_context(nc.sbuf_tensor("expert_f", [P, TILES], F32)),
            "expert_i": ctx.enter_context(nc.sbuf_tensor("expert_i", [P, TILES], I32)),
            "offset_i": ctx.enter_context(nc.sbuf_tensor("offset_i", [P, TILES], I32)),
            "ident16": ctx.enter_context(nc.sbuf_tensor("ident16", [P, P], F16)),
            "b1": ctx.enter_context(nc.sbuf_tensor("b1", [P, E * HC], F32)),
        }
        keep["cw"] = keep["m8"][:, 0:NB * S * 2]
        build_attend(nc, io, keep)
        build_experts(nc, io, keep)
        build_combine(nc, io, keep)


def kernel(**inputs):
    import numpy as np
    import concourse.bacc as bacc
    from concourse.bass_utils import run_bass_kernel_spmd

    x = inputs["L0_attn_x"].reshape(TOKENS, D)
    arrays = {
        "xT": x.reshape(NB, BLK, DC, P).transpose(0, 3, 2, 1).reshape(NB, P, DC * BLK),
        "x_tok": x.reshape(NB, S, P, D).transpose(0, 2, 1, 3),
        "wa": np.stack([inputs[f"L0_attn_{n}"].T.reshape(DC, P, D) for n in ("Wq", "Wv", "Wg", "Wo")], axis=2),
        "wf": np.stack([inputs["L0_ffn_W1"].reshape(E, DC, P, HID).transpose(0, 2, 1, 3).reshape(E, P, DC * HID),
                        inputs["L0_ffn_W2"].reshape(E, HC, P, D).transpose(0, 2, 1, 3).reshape(E, P, HC * D)],
                       axis=1).reshape(2 * E, P, DC * HID),
        "b1": inputs["L0_ffn_b1"].reshape(E * HC, P).T,
        "b2": inputs["L0_ffn_b2"].reshape(E * D),
        "gate_w": inputs["L0_ffn_gate_W"].reshape(DC, P, E).transpose(1, 0, 2),
        "ln_gb": np.stack([inputs["L0_attn_ln_g"].reshape(DC, P), inputs["L0_attn_ln_b"].reshape(DC, P)]).transpose(2, 0, 1),
        "lam": np.repeat(inputs["L0_attn_decay"][:, 1, 0], D // 16).reshape(DC, P).T,
        "ident": np.eye(P, dtype=np.float32),
        "ident16": np.eye(P, dtype=np.float16),
        "tri_ones": np.stack([np.triu(np.ones((P, P), np.float16), 1), np.ones((P, P), np.float16)], axis=1),
        "iota_e": np.tile(np.arange(E, dtype=np.float32), (P, 1)),
        "region_base": np.tile(np.arange(E, dtype=np.float32) * REGION, (P, 1)),
        "tile_iota": np.tile(np.arange(TILES, dtype=np.float32), (P, 1)),
        "token0": (np.arange(P)[:, None] + P * np.arange(S)[None, :]).astype(np.float32),
        "keep_state": np.tile((np.arange(NB + 1) % BLOCKS_PER_SEQ != 0).astype(np.float32), (P, 1)),
    }
    arrays = {n: np.ascontiguousarray(a) for n, a in arrays.items()}
    nc = bacc.Bacc("TRN2", target_bir_lowering=False, num_devices=1)
    io = {n: nc.dram_tensor(n + "_in", a.shape, mybir.dt.from_np(a.dtype), kind="ExternalInput").ap()
          for n, a in arrays.items()}
    io["out"] = nc.dram_tensor("out", [TOKENS, D], F32, kind="ExternalOutput").ap()
    build(nc, io)
    r = run_bass_kernel_spmd(nc, [{n + "_in": a for n, a in arrays.items()}], core_ids=[0])
    return r.results[0]["out"].reshape(inputs["L0_attn_x"].shape)
```

```python
from contextlib import ExitStack

import concourse.bass as bass
from concourse import mybir

F32 = mybir.dt.float32
F16 = mybir.dt.float16
U32 = mybir.dt.uint32
I32 = mybir.dt.int32
ALU = mybir.AluOpType
ACT = mybir.ActivationFunctionType
AX_X = mybir.AxisListType.X

P = 128
D = 256
DC = D // P
E = 8
HID = 512
HC = HID // P
TOKENS = 8192
BLK = 512
NB = TOKENS // BLK
BLOCKS_PER_SEQ = 8
S = BLK // P
TILE = 256
TS = TILE // P
REGION = TOKENS + TILE
TILES = (2 * TOKENS + E * (TILE - 1)) // TILE
ROW = 264
META = D
NO_TOKEN = 20000.0
WSCALE = 64.0
LN_EPS = 1e-05
W_Q, W_V, W_G, W_O = range(4)


def wait(eng, sem, value, beside=None):
    if not isinstance(value, int) or value > 0:
        if beside is not None and not isinstance(value, int):
            eng.wait_ge(*beside)
        eng.wait_ge(sem, value)


def build_attend(nc, io, keep):
    x1, wf16, m8, cw = keep["x1"], keep["wf16"], keep["m8"], keep["cw"]
    expert_f, expert_i, offset_i = keep["expert_f"], keep["expert_i"], keep["offset_i"]
    region = io["region"]
    with ExitStack() as ctx:
        def sb(name, shape, dt):
            return ctx.enter_context(nc.sbuf_tensor(name, shape, dt))

        def sem(name):
            return ctx.enter_context(nc.semaphore(name))

        ident = keep["ident"]
        tri_ones = sb("tri_ones", [P, 2, P], F16)
        count_acc = sb("count_acc", [P, E], F16)
        iota_e = sb("iota_e", [P, E], F32)
        region_base = sb("region_base", [P, E], F32)
        token0 = sb("token0", [P, S], F32)
        tile_iota = sb("tile_iota", [P, TILES], F32)
        keep_state = sb("keep_state", [P, NB + 1], F32)
        half_pow = sb("half_pow", [P, S], F32)
        eps = sb("eps", [P, S], F32)
        minus_one = sb("minus_one", [P, S], F32)
        blk = sb("blk", [P, S], F32)
        ones_e = sb("ones_e", [P, E], F32)
        lam = sb("lam", [P, DC], F32)
        ln_gb = sb("ln_gb", [P, 2, DC], F32)
        gate_w = sb("gate_w", [P, DC, E], F32)
        wa_hi = sb("wa_hi", [P, 4, DC, D], F16)
        wa_lo = sb("wa_lo", [P, 4, DC, D], F16)
        xT32 = [sb(f"xT32_{u}", [P, DC * BLK], F32) for u in range(2)]
        xT_hi = [sb(f"xT_hi_{u}", [P, DC, BLK], F16) for u in range(2)]
        xT_lo = [sb(f"xT_lo_{u}", [P, DC, BLK], F16) for u in range(2)]
        x_tok = [sb(f"x_tok_{u}", [P, S * D], F32) for u in range(2)]
        carry = sb("carry", [P, DC], F32)
        state = sb("state", [P, BLK], F32)
        y = sb("y", [P, DC, BLK], F32)
        gate = [sb(f"gate_{u}", [P, DC * BLK], F32) for u in range(2)]
        yn = sb("yn", [P, DC * BLK], F32)
        wa32 = [t[:, :].rearrange("p (w d) -> p w d", w=4) for t in (gate[1], yn)]
        z_hi = sb("z_hi", [P, DC, BLK], F16)
        z_lo = sb("z_lo", [P, DC, BLK], F16)
        row = [sb(f"row_{u}", [P, S, ROW], F32) for u in range(2)]
        x1T = sb("x1T", [P, DC * BLK], F32)
        wf32 = sb("wf32", [P, DC * HID], F32)
        bn_y = sb("bn_y", [P, S, 6], F32)
        mv_y = sb("mv_y", [P, S, 2], F32)
        rs_y = sb("rs_y", [P, 3, S], F32)
        bn_x = sb("bn_x", [P, S, 6], F32)
        mv_x = sb("mv_x", [P, S, 2], F32)
        rs_x = sb("rs_x", [P, 3, S], F32)
        logits = sb("logits", [P, S, E], F32)
        m8_new = sb("m8_new", [P, S, E], F32)
        i8 = sb("i8", [P, S, E], U32)
        chosen = sb("chosen", [P, 2, S], F32)
        onehot = sb("onehot", [P, 2, S, E], F32)
        mask = sb("mask", [P, S, E], F16)
        block_sum = sb("block_sum", [P, E], F32)
        position = sb("position", [P, S, E], F32)
        picked = sb("picked", [P, 2, S, E], F32)
        slot = [sb(f"slot_{u}", [P, 2, S], U32) for u in range(2)]
        token = sb("token", [P, S], F32)

        ps_a = ctx.enter_context(nc.psum_tensor("ps_a", [P, 3 * BLK], F32))
        ps_b = ctx.enter_context(nc.psum_tensor("ps_b", [P, 3 * BLK], F32))
        ps_t = ctx.enter_context(nc.psum_tensor("ps_t", [P, 2 * BLK], F32))
        vqg = [ps_a, ps_b]
        ps_n = ps_t[:, 0:E]
        yT = ps_a[:, 0:2 * BLK]
        ps_logits = ps_a[:, 2 * BLK:2 * BLK + S * E]
        ps_pos = ps_a[:, 2 * BLK + 64:2 * BLK + 64 + S * E]

        par_in = sem("par_in")
        wa_in = [sem("wa_in_0"), sem("wa_in_1")]
        xT_in = [sem("xT_in_0"), sem("xT_in_1")]
        xtok_in = [sem("xtok_in_0"), sem("xtok_in_1")]
        wf_in = sem("wf_in")
        x1_kept = [sem("x1_kept_0"), sem("x1_kept_1")]
        scattered = [sem("scattered_0"), sem("scattered_1")]
        set_done = sem("set_done")
        wa_hi_done = sem("wa_hi_done")
        wa_lo_done = sem("wa_lo_done")
        x_hi = sem("x_hi")
        x_lo = sem("x_lo")
        projected = sem("projected")
        silu_done = sem("silu_done")
        scanned = sem("scanned")
        y_done = sem("y_done")
        carried = sem("carried")
        y_by_token = sem("y_by_token")
        bn_y_done = sem("bn_y_done")
        stats_y = sem("stats_y")
        rstd_y_step = sem("rstd_y_step")
        rstd_y = sem("rstd_y")
        bn_x_done = sem("bn_x_done")
        stats_x = sem("stats_x")
        rstd_x_step = sem("rstd_x_step")
        rstd_x = sem("rstd_x")
        y_normed = sem("y_normed")
        yn_by_channel = sem("yn_by_channel")
        affine = sem("affine")
        z_done = sem("z_done")
        zhi_done = sem("zhi_done")
        zlo_done = sem("zlo_done")
        out_projected = sem("out_projected")
        residual = sem("residual")
        x1_done = sem("x1_done")
        x1_by_channel = sem("x1_by_channel")
        x1T_done = sem("x1T_done")
        routed = sem("routed")
        top_done = sem("top_done")
        logits_read = sem("logits_read")
        top_kept = sem("top_kept")
        index_done = sem("index_done")
        chosen_done = sem("chosen_done")
        onehot_done = sem("onehot_done")
        mask_done = sem("mask_done")
        summed = sem("summed")
        counted = sem("counted")
        pos_done = sem("pos_done")
        pos_read = sem("pos_read")
        picked_done = sem("picked_done")
        slots_done = sem("slots_done")
        meta_done = sem("meta_done")
        token_next = sem("token_next")
        wf_scaled = sem("wf_scaled")
        wf_hi_done = sem("wf_hi_done")
        wf_lo_done = sem("wf_lo_done")

        slots_of = sb("slots_of", [P, E], F32)
        tiles_i = sb("tiles_i", [P, E], I32)
        tiles_of = sb("tiles_of", [P, E], F32)
        tiles_to = sb("tiles_to", [P, E], F32)
        skip_rows = sb("skip_rows", [P, E], F32)
        tail_f = sb("tail_f", [P, E], F32)
        tail_i = sb("tail_i", [P, E], I32)
        NT = NB * S
        at = TS * ROW
        blank = gate[0][:, 0:at].rearrange("p (s w) -> p s w", s=TS)
        offset_f = gate[0][:, at:at + TILES]
        total = gate[0][:, at + TILES:at + TILES + NT]
        inv = gate[0][:, at + TILES + NT:at + TILES + 2 * NT]
        behind = gate[1][:, 0:TILES * E].rearrange("p (t e) -> p t e", e=E)
        prob = gate[1][:, TILES * E:TILES * E + 2 * NT].rearrange("p (t k) -> p t k", k=2)
        skipped = yn[:, 0:TILES * E].rearrange("p (t e) -> p t e", e=E)
        dif = x1T[:, 0:NT * E].rearrange("p (t e) -> p t e", e=E)
        total_slots = sem("total_slots")
        tail_done = sem("tail_done")
        table_step = sem("table_step")
        blanked = sem("blanked")
        dif_done = sem("dif_done")
        exp_done = sem("exp_done")

        N_PAR = 11

        def pipeline(eng, step):
            for i in range(4):
                step(i // 2, i % 2, True, i >= 1, i >= 2, i >= 3)
            with eng.Fori(2, NB // 2 - 1) as j:
                for u in range(2):
                    step(j, u, True, True, True, True)
            for u in range(2):
                step(NB // 2 - 1, u, True, True, True, True)
            step(NB // 2, 0, False, True, True, True)
            step(NB // 2, 1, False, False, True, True)
            step(NB // 2 + 1, 0, False, False, False, True)

        def x1_by(now):
            return ps_t if now else ps_b

        block = ctx.enter_context(nc.Block())

        @block.sync
        def _(sp):
            def keep_x1(b, u):
                sp.dma_start(x1[:, bass.ds(b * S * D, S * D)].rearrange("p (s d) -> p s d", s=S),
                             row[u][:, :, 0:D]).then_inc(x1_kept[u], 16)

            def load(j, u):
                i = 2 * j + u
                wait(sp, x_hi, i - 1)
                wait(sp, x_lo, i - 1)
                sp.dma_start(xT32[u][:, :], io["xT"][i]).then_inc(xT_in[u], 16)
                if not (isinstance(i, int) and i == 0):
                    load_tokens(i - 1, 1 - u)

            def load_tokens(b, u):
                wait(sp, x1_done, b - 1)
                sp.dma_start(x_tok[u][:, :].rearrange("p (s d) -> p s d", s=S),
                             io["x_tok"][b]).then_inc(xtok_in[u], 16)
                if not (isinstance(b, int) and b < 2):
                    keep_x1(b - 2, u)

            load(0, 0)
            for dst, src in ((lam[:, :], io["lam"]), (keep_state[:, :], io["keep_state"]),
                             (ln_gb[:, :, :], io["ln_gb"]),
                             (tri_ones[:, :, :], io["tri_ones"]), (iota_e[:, :], io["iota_e"]),
                             (region_base[:, :], io["region_base"]), (token0[:, :], io["token0"]),
                             (gate_w[:, :, :], io["gate_w"]), (tile_iota[:, :], io["tile_iota"]),
                             (keep["ident"][:, :], io["ident"]), (keep["b1"][:, :], io["b1"])):
                sp.dma_start(dst, src).then_inc(par_in, 16)
            for i in range(1, 4):
                load(i // 2, i % 2)
            with sp.Fori(2, NB // 2) as j:
                for u in range(2):
                    load(j, u)
            load_tokens(NB - 1, 1)
            for u in range(2):
                sp.wait_ge(x1_done, NB - 1 + u)
                keep_x1(NB - 2 + u, u)
            sp.wait_ge(tail_done, 1)
            for e in range(E):
                first = sp.value_load(tail_i[0:1, e:e + 1], min_val=0, max_val=E * REGION - TILE)
                sp.dma_start(region[bass.ds(first, TILE), :].rearrange("(s p) w -> p s w", p=P),
                             blank).then_inc(blanked, 16)
            sp.dma_start(region[E * REGION:E * REGION + TILE, :].rearrange("(s p) w -> p s w", p=P),
                         blank).then_inc(blanked, 16)
            for u in range(2):
                sp.wait_ge(x1_kept[u], 16 * NB // 2)
            sp.wait_ge(blanked, 16 * (E + 1))

        @block.tensor
        def _(pe):
            pe.wait_ge(wa_lo_done, 2)

            def project(u, c, parts):
                for n in parts:
                    w = (W_V, W_Q, W_G)[n]
                    dst = vqg[c][:, n * BLK:(n + 1) * BLK]
                    m = 0
                    for k in range(DC):
                        for a, b in ((wa_hi, xT_hi[u]), (wa_lo, xT_hi[u]), (wa_hi, xT_lo[u])):
                            last = nc.tensor.matmul(dst, a[:, w, k, c * P:(c + 1) * P], b[:, k, :],
                                                    start=(m == 0), stop=(m == 3 * DC - 1))
                            m += 1
                if 2 in parts:
                    last.then_inc(projected, 1)

            def enter(i, u):
                wait(pe, x_hi, i + 1)
                wait(pe, x_lo, i + 1)
                wait(pe, y_done, 2 * i - 1)
                project(u, 1, (0,))

            enter(0, 0)
            project(0, 1, (1, 2))
            pe.wait_ge(par_in, 16 * N_PAR)
            pe.wait_ge(set_done, 1)

            def transpose_x1(i, u, now):
                wait(pe, x1_done, i - 1)
                if now:
                    wait(pe, residual, i)
                else:
                    wait(pe, y_done, 2 * NB)
                    wait(pe, silu_done, 2 * NB)
                    wait(pe, x1T_done, i - 2)
                for c in range(DC):
                    for s in range(S):
                        last = nc.tensor.transpose(
                            x1_by(now)[:, c * BLK + s * P:c * BLK + (s + 1) * P],
                            row[u][:, s, c * P:(c + 1) * P], ident[:, :])
                last.then_inc(x1_by_channel, 1)

            def step(j, u, now, prev, prev2, prev3):
                i = 2 * j + u
                more = now and not (isinstance(i, int) and i == NB - 1)
                if prev:
                    wait(pe, y_normed, i)
                    wait(pe, residual, i - 1)
                    for c in range(DC):
                        for s in range(S):
                            last = nc.tensor.transpose(
                                ps_t[:, c * BLK + s * P:c * BLK + (s + 1) * P],
                                yn[:, s * D + c * P:s * D + (c + 1) * P], ident[:, :])
                    last.then_inc(yn_by_channel, 1)
                if now:
                    wait(pe, silu_done, 2 * i)
                    project(u, 0, (0, 1))
                if prev3:
                    wait(pe, mask_done, i - 2)
                    wait(pe, counted, i - 3)
                    for s in range(S):
                        dst = ps_pos[:, s * E:(s + 1) * E]
                        nc.tensor.matmul(dst, tri_ones[:, 0, :], mask[:, s, :], start=True, stop=False)
                        for before in range(s):
                            nc.tensor.matmul(dst, tri_ones[:, 1, :], mask[:, before, :], start=False, stop=False)
                        last = nc.tensor.matmul(dst, tri_ones[:, 1, :], count_acc[:, :], start=False, stop=True)
                    last.then_inc(pos_done, 1)
                if now:
                    if prev3:
                        wait(pe, pos_read, i - 2)
                    project(u, 0, (2,))
                if prev:
                    wait(pe, zlo_done, 2 * i - 1)
                    for s in range(S):
                        m = 0
                        for c in range(DC):
                            for a, b in ((z_hi, wa_hi), (z_hi, wa_lo), (z_lo, wa_hi)):
                                if s == 0 and c == 1 and m == 3:
                                    wait(pe, zhi_done, 2 * i)
                                if s == 0 and c == 1 and a is z_lo:
                                    wait(pe, zlo_done, 2 * i)
                                last = nc.tensor.matmul(ps_t[:, s * D:(s + 1) * D], a[:, c, s * P:(s + 1) * P],
                                                        b[:, W_O, c, :], start=(m == 0), stop=(m == 3 * DC - 1))
                                m += 1
                    last.then_inc(out_projected, 1)
                if now:
                    wait(pe, y_done, 2 * i + 2)
                    for s in range(S):
                        for c in range(DC):
                            last = nc.tensor.transpose(yT[:, s * D + c * P:s * D + (c + 1) * P],
                                                       y[:, c, s * P:(s + 1) * P], ident[:, :])
                    last.then_inc(y_by_token, 1)
                if more:
                    enter(i + 1, 1 - u)
                if prev2:
                    transpose_x1(i, u, now)
                if more:
                    wait(pe, silu_done, 2 * i + 1)
                    project(1 - u, 1, (1, 2))
                if prev2:
                    wait(pe, x1T_done, i - 1)
                    if now:
                        wait(pe, silu_done, 2 * i + 2)
                    else:
                        wait(pe, pos_read, i - 2)
                    for s in range(S):
                        for c in range(DC):
                            last = nc.tensor.matmul(ps_logits[:, s * E:(s + 1) * E],
                                                    x1T[:, c * BLK + s * P:c * BLK + (s + 1) * P],
                                                    gate_w[:, c, :], start=(c == 0), stop=(c == DC - 1))
                    last.then_inc(routed, 1)

            pipeline(pe, step)
            pe.wait_ge(counted, NB)
            nc.tensor.matmul(ps_n, tri_ones[:, 1, :], count_acc[:, :], start=True,
                             stop=True).then_inc(total_slots, 1)

        @block.vector
        def _(dve):
            v = nc.vector
            v.memset(carry[:, :], 0.0)
            v.memset(count_acc[:, :], 0.0)
            v.memset(half_pow[:, :], -0.5)
            v.memset(eps[:, :], LN_EPS)
            v.memset(minus_one[:, :], -1.0)
            v.memset(blk[:, :], float(BLK))
            v.memset(ones_e[:, :], 1.0)
            for u in range(2):
                last = v.memset(row[u][:, :, :], 0.0)
            last.then_inc(set_done, 1)
            for h in range(2):
                dve.wait_ge(wa_hi_done, h + 1)
                v.scalar_tensor_tensor(out=wa_lo[:, :, h, :], in0=wa32[h], scalar=WSCALE,
                                       in1=wa_hi[:, :, h, :], op0=ALU.mult,
                                       op1=ALU.subtract).then_inc(wa_lo_done, 1)

            dve.wait_ge(par_in, 16 * N_PAR)

            def split_x(b, u):
                wait(dve, x_hi, b + 1)
                wait(dve, projected, 2 * b - 2)
                v.tensor_tensor(xT_lo[u][:, :, :], xT32[u][:, :].rearrange("p (c t) -> p c t", c=DC),
                                xT_hi[u][:, :, :], ALU.subtract).then_inc(x_lo, 1)

            def retain(i, u, c):
                n = 1 - c
                wait(dve, projected, 2 * i + n + 1)
                wait(dve, carried, 2 * i + n - 1)
                wait(dve, y_done, 2 * i + n)
                v.tensor_tensor_scan(state[:, :], lam[:, c:c + 1].broadcast_to([P, BLK]),
                                     vqg[c][:, 0:BLK], carry[:, c:c + 1], ALU.mult,
                                     ALU.add).then_inc(scanned, 1)
                wait(dve, scanned, 2 * i + n + 1)
                v.tensor_scalar(carry[:, c:c + 1], state[:, BLK - 1:BLK], keep_state[:, bass.ds(i + 1, 1)], None,
                                ALU.mult).then_inc(carried, 1)
                if n == 0:
                    wait(dve, y_by_token, i)
                v.scalar_tensor_tensor(out=y[:, c, :], in0=vqg[c][:, BLK:2 * BLK],
                                       scalar=1.0 / (WSCALE * WSCALE), in1=state[:, :],
                                       op0=ALU.mult, op1=ALU.mult).then_inc(y_done, 1)

            split_x(0, 0)

            def step(j, u, now, prev, prev2, prev3):
                i = 2 * j + u
                b = i - 2
                if now:
                    retain(i, u, 1)
                if prev3:
                    wait(dve, routed, i - 2)
                    wait(dve, top_kept, b - 1)
                    v.tensor_copy(logits[:, :, :], ps_logits.rearrange("p (s e) -> p s e", s=S)
                                  ).then_inc(logits_read, 1)
                    wait(dve, logits_read, i - 2, beside=(set_done, 1))
                    for s in range(S):
                        last = v.max(m8_new[:, s, :], logits[:, s, :])
                    last.then_inc(top_done, 1)
                    wait(dve, top_done, i - 2, beside=(set_done, 1))
                    for s in range(S):
                        last = v.max_index(i8[:, s, :], m8_new[:, s, :], logits[:, s, :])
                    last.then_inc(index_done, 1)
                    wait(dve, index_done, i - 2)
                    wait(dve, meta_done, b - 1)
                    v.tensor_copy(chosen[:, :, :], i8[:, :, 0:2].rearrange("p s k -> p k s")
                                  ).then_inc(chosen_done, 1)
                    wait(dve, chosen_done, i - 2)
                    v.tensor_tensor(onehot[:, :, :, :],
                                    iota_e[:, :].unsqueeze(1).unsqueeze(1).broadcast_to([P, 2, S, E]),
                                    chosen[:, :, :].unsqueeze(3).broadcast_to([P, 2, S, E]),
                                    ALU.is_equal).then_inc(onehot_done, 1)
                    wait(dve, onehot_done, i - 2)
                    v.tensor_tensor(mask[:, :, :], onehot[:, 0, :, :], onehot[:, 1, :, :],
                                    ALU.add).then_inc(mask_done, 1)
                    wait(dve, mask_done, i - 2)
                    v.tensor_reduce(block_sum[:, :], mask[:, :, :].rearrange("p s e -> p e s"), AX_X,
                                    ALU.add).then_inc(summed, 1)
                if prev:
                    wait(dve, silu_done, 2 * i)
                    for c in range(DC):
                        half = slice(c * BLK, (c + 1) * BLK)
                        wait(dve, affine, 2 * i - 1 + c)
                        v.tensor_tensor(yn[:, half], yn[:, half], gate[1 - u][:, half], ALU.mult).then_inc(z_done, 1)
                if prev3:
                    wait(dve, pos_done, b)
                    v.tensor_tensor(position[:, :, :], ps_pos.rearrange("p (s e) -> p s e", s=S),
                                    region_base[:, :].unsqueeze(1).broadcast_to([P, S, E]),
                                    ALU.add).then_inc(pos_read, 1)
                    wait(dve, summed, b)
                    v.tensor_tensor(count_acc[:, :], count_acc[:, :], block_sum[:, :], ALU.add).then_inc(counted, 1)
                    wait(dve, pos_read, b)
                    v.tensor_tensor(picked[:, :, :, :], onehot[:, :, :, :],
                                    position[:, :, :].unsqueeze(1).broadcast_to([P, 2, S, E]),
                                    ALU.mult).then_inc(picked_done, 1)
                    wait(dve, picked_done, b)
                    with nc.allow_low_precision("row numbers are whole and below 2^24"):
                        v.tensor_reduce(slot[1 - u][:, :, :], picked[:, :, :, :], AX_X, ALU.add).then_inc(slots_done, 1)
                if prev:
                    wait(dve, out_projected, i - 1)
                    for c in range(DC):
                        wait(dve, zhi_done, 2 * i - 1 + c)
                        v.tensor_tensor(z_lo[:, c, :], yn[:, c * BLK:(c + 1) * BLK], z_hi[:, c, :],
                                        ALU.subtract).then_inc(zlo_done, 1)
                if now:
                    retain(i, u, 0)
                    if not (isinstance(i, int) and i == NB - 1):
                        split_x(i + 1, 1 - u)
                if prev:
                    wait(dve, out_projected, i)
                    wait(dve, xtok_in[1 - u], 16 * (j + u))
                    t = x_tok[1 - u]
                    v.scalar_tensor_tensor(out=t[:, :], in0=ps_t[:, :], scalar=1.0 / WSCALE, in1=t[:, :],
                                           op0=ALU.mult, op1=ALU.add).then_inc(residual, 1)
                if now:
                    wait(dve, rstd_y, i)
                    wait(dve, y_by_token, i + 1)
                    for s in range(S):
                        last = v.bn_stats(bn_y[:, s, :], yT[:, s * D:(s + 1) * D])
                    last.then_inc(bn_y_done, 1)
                    wait(dve, bn_y_done, i + 1, beside=(set_done, 1))
                    for s in range(S):
                        last = v.bn_aggr(mv_y[:, s, :], bn_y[:, s, :])
                    last.then_inc(stats_y, 1)
                if prev:
                    wait(dve, rstd_x, i - 1)
                    wait(dve, residual, i)
                    for s in range(S):
                        last = v.bn_stats(bn_x[:, s, :], t[:, s * D:(s + 1) * D])
                    last.then_inc(bn_x_done, 1)
                    wait(dve, bn_x_done, i, beside=(set_done, 1))
                    for s in range(S):
                        last = v.bn_aggr(mv_x[:, s, :], bn_x[:, s, :])
                    last.then_inc(stats_x, 1)

            pipeline(dve, step)

            steps = [0]

            def link(ins):
                steps[0] += 1
                ins.then_inc(table_step, 1)
                dve.wait_ge(table_step, steps[0])

            link(v.memset(blank, 0.0))
            v.memset(blank[:, :, META], NO_TOKEN)
            v.memset(blank[:, :, META + 1], -1.0)
            dve.wait_ge(total_slots, 1)
            link(v.tensor_copy(slots_of[:, :], ps_n))
            v.tensor_scalar(tiles_i[:, :], slots_of[:, :], float(TILE - 1), None, ALU.add)
            link(v.tensor_tensor(tail_f[:, :], region_base[:, :], slots_of[:, :], ALU.add))
            v.tensor_copy(tail_i[:, :], tail_f[:, :]).then_inc(tail_done, 1)
            link(v.tensor_scalar(tiles_i[:, :], tiles_i[:, :], TILE.bit_length() - 1, None, ALU.arith_shift_right))
            link(v.tensor_copy(tiles_of[:, :], tiles_i[:, :]))
            v.tensor_scalar(skip_rows[:, :], tiles_of[:, :], -float(TILE), float(REGION), ALU.mult, ALU.add)
            link(v.tensor_tensor_scan(tiles_to[:, :], ones_e[:, :], tiles_of[:, :], 0.0, ALU.mult, ALU.add))
            v.tensor_scalar(offset_f, tile_iota[:, :], float(TILE), None, ALU.mult)
            link(v.tensor_tensor(behind, tile_iota[:, :].unsqueeze(2).broadcast_to([P, TILES, E]),
                                 tiles_to[:, :].unsqueeze(1).broadcast_to([P, TILES, E]), ALU.is_ge))
            v.tensor_reduce(expert_f[:, :], behind, AX_X, ALU.add)
            link(v.tensor_tensor(skipped, behind, skip_rows[:, :].unsqueeze(1).broadcast_to([P, TILES, E]), ALU.mult))
            link(v.tensor_reduce(behind[:, :, 0], skipped, AX_X, ALU.add))
            v.tensor_scalar(expert_f[:, :], expert_f[:, :], float(E - 1), None, ALU.min)
            link(v.tensor_tensor(offset_f, offset_f, behind[:, :, 0], ALU.add))
            v.tensor_scalar(offset_i[:, :], offset_f, float(E * REGION), None, ALU.min)
            link(v.tensor_copy(expert_i[:, :], expert_f[:, :]))

            dve.wait_ge(top_kept, NB)
            m8v = m8[:, :].rearrange("p (t e) -> p t e", e=E)
            v.tensor_tensor(dif, m8v, m8v[:, :, 0:1].broadcast_to([P, NT, E]), ALU.subtract).then_inc(dif_done, 1)
            dve.wait_ge(exp_done, 1)
            link(v.tensor_reduce(total, dif, AX_X, ALU.add))
            link(v.reciprocal(inv, total))
            link(v.tensor_tensor(prob, dif[:, :, 0:2], inv.unsqueeze(2).broadcast_to([P, NT, 2]), ALU.mult))
            link(v.tensor_tensor(total, prob[:, :, 0], prob[:, :, 1], ALU.add))
            link(v.tensor_scalar(total, total, 1e-8, 2.0, ALU.add, ALU.mult))
            link(v.reciprocal(inv, total))
            link(v.tensor_tensor(cw[:, :].rearrange("p (t k) -> p t k", k=2), prob,
                                 inv.unsqueeze(2).broadcast_to([P, NT, 2]), ALU.mult))

        @block.scalar
        def _(act):
            a = nc.scalar
            for h in range(2):
                act.dma_start(wa32[h], io["wa"][h]).then_inc(wa_in[h], 16)
            for h in range(2):
                act.wait_ge(wa_in[h], 16)
                a.activation(wa_hi[:, :, h, :], wa32[h], ACT.Copy, scale=WSCALE).then_inc(wa_hi_done, 1)

            def split_x(b, u, loads):
                wait(act, xT_in[u], 16 * loads)
                wait(act, projected, 2 * b - 2)
                a.activation(xT_hi[u][:, :, :], xT32[u][:, :].rearrange("p (c t) -> p c t", c=DC),
                             ACT.Copy).then_inc(x_hi, 1)

            split_x(0, 0, 1)

            def step(j, u, now, prev, prev2, prev3):
                i = 2 * j + u
                if now:
                    wait(act, projected, 2 * i + 1)
                    wait(act, z_done, 2 * i - 2)
                    a.activation(gate[u][:, BLK:2 * BLK], ps_b[:, 2 * BLK:3 * BLK], ACT.Silu,
                                 scale=1.0 / WSCALE).then_inc(silu_done, 1)
                if prev:
                    wait(act, yn_by_channel, i)
                    wait(act, par_in, 16 * N_PAR)
                    for c in range(DC):
                        a.activation(yn[:, c * BLK:(c + 1) * BLK], ps_t[:, c * BLK:(c + 1) * BLK], ACT.Identity,
                                     scale=ln_gb[:, 0, c:c + 1], bias=ln_gb[:, 1, c:c + 1]).then_inc(affine, 1)
                    wait(act, wf_in, 16 * i)
                    a.activation(wf32[:, :], wf32[:, :], ACT.Copy, scale=WSCALE).then_inc(wf_scaled, 1)
                    wait(act, out_projected, i - 1)
                    for c in range(DC):
                        wait(act, z_done, 2 * i - 1 + c)
                        a.activation(z_hi[:, c, :], yn[:, c * BLK:(c + 1) * BLK], ACT.Copy).then_inc(zhi_done, 1)
                    wait(act, wf_scaled, i)
                    a.activation(wf16[:, bass.ds((i - 1) * 2 * DC * HID, DC * HID)], wf32[:, :],
                                 ACT.Copy).then_inc(wf_hi_done, 1)
                if now:
                    wait(act, projected, 2 * i + 2)
                    a.activation(gate[u][:, 0:BLK], ps_a[:, 2 * BLK:3 * BLK], ACT.Silu,
                                 scale=1.0 / WSCALE).then_inc(silu_done, 1)
                    if not (isinstance(i, int) and i == NB - 1):
                        split_x(i + 1, 1 - u, j + u + 1)
                if prev2:
                    wait(act, rstd_x, i - 1)
                    wait(act, x1_by_channel, i - 3)
                    wait(act, scattered[u], 128 * (j - 1))
                    wait(act, x1_kept[u], 16 * (j - 1))
                    wait(act, set_done, 1)
                    for s in range(S):
                        last = a.activation(row[u][:, s, 0:D], x_tok[u][:, s * D:(s + 1) * D],
                                            ACT.Identity, scale=rs_x[:, 1, s:s + 1], bias=rs_x[:, 2, s:s + 1])
                    last.then_inc(x1_done, 1)
                    wait(act, x1_by_channel, i - 1)
                    wait(act, routed, i - 2)
                    a.activation(x1T[:, :], x1_by(now)[:, 0:2 * BLK], ACT.Copy).then_inc(x1T_done, 1)
                if now:
                    wait(act, wf_lo_done, i)
                    act.dma_start(wf32[:, :], io["wf"][i]).then_inc(wf_in, 16)
                    wait(act, rstd_y, i + 1)
                    wait(act, zlo_done, 2 * i)
                    for s in range(S):
                        last = a.activation(yn[:, s * D:(s + 1) * D], yT[:, s * D:(s + 1) * D], ACT.Identity,
                                            scale=rs_y[:, 1, s:s + 1], bias=rs_y[:, 2, s:s + 1])
                    last.then_inc(y_normed, 1)

            pipeline(act, step)
            act.wait_ge(dif_done, 1)
            a.activation(dif, dif, ACT.Exp).then_inc(exp_done, 1)

        @block.gpsimd
        def _(pool):
            g = nc.gpsimd
            pool.wait_ge(par_in, 16 * N_PAR)
            pool.wait_ge(set_done, 1)
            zeros_set = (set_done, 1)

            g.tensor_copy(token[:, :], token0[:, :]).then_inc(token_next, 1)

            def rstd(mv, rs, stepped, done, n):
                g.tensor_tensor(rs[:, 2, :], mv[:, :, 0], minus_one[:, :], ALU.mult)
                g.tensor_tensor(rs[:, 0, :], mv[:, :, 1], eps[:, :], ALU.add).then_inc(stepped, 1)
                wait(pool, stepped, 2 * n + 1)
                g.tensor_tensor(rs[:, 1, :], rs[:, 0, :], half_pow[:, :], ALU.pow).then_inc(stepped, 1)
                wait(pool, stepped, 2 * n + 2)
                g.tensor_tensor(rs[:, 2, :], rs[:, 2, :], rs[:, 1, :], ALU.mult).then_inc(done, 1)

            def split_weights(i):
                wait(pool, wf_hi_done, i)
                base = (i - 1) * 2 * DC * HID
                g.tensor_tensor(wf16[:, bass.ds(base + DC * HID, DC * HID)], wf32[:, :],
                                wf16[:, bass.ds(base, DC * HID)], ALU.subtract).then_inc(wf_lo_done, 1)

            def scatter(u, k):
                for s in range(S):
                    g.indirect_dma_start(region, bass.IndirectOffsetOnAxis(slot[u][:, k, s:s + 1], 0),
                                         row[u][:, s, :], None).then_inc(scattered[u], 16)

            def step(j, u, now, prev, prev2, prev3):
                i = 2 * j + u
                b = i - 2
                if prev3:
                    wait(pool, chosen_done, b, beside=zeros_set)
                    g.tensor_copy(m8[:, bass.ds((b - 1) * S * E, S * E)],
                                  m8_new[:, :, :].rearrange("p s e -> p (s e)")).then_inc(top_kept, 1)
                    wait(pool, x1_done, b, beside=zeros_set)
                    wait(pool, token_next, b, beside=zeros_set)
                    g.tensor_copy(row[1 - u][:, :, META], token[:, :])
                    g.tensor_copy(row[1 - u][:, :, META + 1], chosen[:, 1, :]).then_inc(meta_done, 1)
                    wait(pool, meta_done, b)
                    g.tensor_tensor(token[:, :], token[:, :], blk[:, :], ALU.add).then_inc(token_next, 1)
                    wait(pool, slots_done, b, beside=zeros_set)
                    wait(pool, x1_done, b, beside=zeros_set)
                    scatter(1 - u, 0)
                if prev and now:
                    split_weights(i)
                if now:
                    wait(pool, stats_y, i + 1)
                    wait(pool, y_normed, i)
                    rstd(mv_y, rs_y, rstd_y_step, rstd_y, i)
                if prev3:
                    scatter(1 - u, 1)
                if prev:
                    wait(pool, stats_x, i)
                    wait(pool, x1_done, i - 1)
                    rstd(mv_x, rs_x, rstd_x_step, rstd_x, i - 1)
                if prev and not now:
                    split_weights(i)

            pipeline(pool, step)
            for u in range(2):
                pool.wait_ge(scattered[u], 128 * NB // 2)


def build_experts(nc, io, keep):
    wf16, expert_f, expert_i, offset_i, ident, b1 = (
        keep[n] for n in ("wf16", "expert_f", "expert_i", "offset_i", "ident", "b1"))
    region, outputs = io["region"], io["outputs"]
    WE = 4 * DC * HID
    with ExitStack() as ctx:
        def sb(name, shape, dt):
            return ctx.enter_context(nc.sbuf_tensor(name, shape, dt))

        def psum(name, shape, dt):
            return ctx.enter_context(nc.psum_tensor(name, shape, dt))

        def sem(name):
            return ctx.enter_context(nc.semaphore(name))

        b2 = sb("b2", [P, E * D], F32)
        rows = [sb(f"rows_{u}", [P, TS, ROW], F32) for u in range(2)]
        xT = [sb(f"xT_{u}", [P, 2 * DC * TILE], F16) for u in range(2)]
        h = [sb(f"h_{u}", [P, HC * TILE], F32) for u in range(2)]
        h_hi = [sb(f"h_hi_{u}", [P, HC * TILE], F16) for u in range(2)]
        h_lo = [sb(f"h_lo_{u}", [P, HC * TILE], F16) for u in range(2)]
        y_out = [sb(f"y_out_{u}", [P, TS * D], F32) for u in range(2)]
        is_second = [sb(f"is_second_{u}", [P, TS], F32) for u in range(2)]
        token = [sb(f"token_of_{u}", [P, TS], F32) for u in range(2)]
        dest_f = sb("dest_f", [P, TS], F32)
        dest = [sb(f"dest_{u}", [P, TS], U32) for u in range(2)]

        ps_x = [psum(f"ps_x_{u}", [P, DC * TILE], F32) for u in range(2)]
        ps_h = [psum(f"ps_h_{u}", [P, HC * TILE], F32) for u in range(2)]
        ps_y = [psum(f"ps_y_{u}", [P, TS * D], F32) for u in range(2)]

        b2_in = sem("b2_in")
        rows_in = [sem("rows_in_0"), sem("rows_in_1")]
        scattered = [sem("y_scattered_0"), sem("y_scattered_1")]
        x_transposed = sem("x_transposed")
        x_hi_done = sem("x_hi_done")
        x_lo_done = sem("x_lo_done")
        hidden = sem("hidden")
        relu_done = sem("relu_done")
        h_hi_done = sem("h_hi_done")
        h_lo_done = sem("h_lo_done")
        projected = sem("y_projected")
        second_done = sem("second_done")
        dest_f_done = sem("dest_f_done")
        dest_done = sem("dest_done")
        y_ready = sem("y_ready")

        def pipeline(eng, step):
            for t in range(4):
                step(t // 2, t % 2, True, True)
            with eng.Fori(2, TILES // 2) as j:
                for u in range(2):
                    step(j, u, True, True)
            step(TILES // 2, 0, True, False)
            step(TILES // 2, 1, False, False)

        assert TILES % 2 == 1
        block = ctx.enter_context(nc.Block())

        @block.sync
        def _(sp):
            def load(j, u):
                t = 2 * j + u
                wait(sp, x_transposed, t - 1)
                wait(sp, second_done, t - 1)
                first = sp.value_load(offset_i[0:1, bass.ds(t, 1)], min_val=0, max_val=E * REGION)
                sp.dma_start(rows[u][:, :, :],
                             region[bass.ds(first, TILE), :].rearrange("(s p) w -> p s w", p=P)
                             ).then_inc(rows_in[u], 16)

            for t in range(4):
                load(t // 2, t % 2)
            with sp.Fori(2, TILES // 2) as j:
                for u in range(2):
                    load(j, u)
            load(TILES // 2, 0)

        @block.tensor
        def _(pe):
            def transpose_rows(t, u, loads):
                wait(pe, rows_in[u], 16 * loads)
                wait(pe, x_lo_done, t - 1)
                for k in range(DC):
                    for s in range(TS):
                        last = nc.tensor.transpose(ps_x[u][:, k * TILE + s * P:k * TILE + (s + 1) * P],
                                                   rows[u][:, s, k * P:(k + 1) * P], ident[:, :])
                last.then_inc(x_transposed, 1)

            transpose_rows(0, 0, 1)

            def step(j, u, now, after):
                t = 2 * j + u
                if now:
                    e = pe.value_load(expert_i[0:1, bass.ds(t, 1)], min_val=0, max_val=E - 1)
                    wait(pe, x_lo_done, t + 1)
                    wait(pe, relu_done, 2 * (t - 1))
                    for c in range(HC):
                        m = 0
                        for k in range(DC):
                            for wl, xl in ((0, 0), (1, 0), (0, 1)):
                                last = nc.tensor.matmul(
                                    ps_h[u][:, c * TILE:(c + 1) * TILE],
                                    wf16[:, bass.ds(e * WE + (wl * DC + k) * HID + c * P, P)],
                                    xT[u][:, (xl * DC + k) * TILE:(xl * DC + k + 1) * TILE],
                                    start=(m == 0), stop=(m == 3 * DC - 1))
                                m += 1
                        if c % 2:
                            last.then_inc(hidden, 1)
                if after:
                    transpose_rows(t + 1, 1 - u, j + u + 1)
                if not (isinstance(t, int) and t == 0):
                    e = pe.value_load(expert_i[0:1, bass.ds(t - 1, 1)], min_val=0, max_val=E - 1)
                    wait(pe, h_lo_done, t)
                    wait(pe, y_ready, t - 2)
                    for s in range(TS):
                        m = 0
                        for k in range(HC):
                            for hl, wl in ((h_hi, 0), (h_lo, 0), (h_hi, 1)):
                                last = nc.tensor.matmul(
                                    ps_y[1 - u][:, s * D:(s + 1) * D],
                                    hl[1 - u][:, k * TILE + s * P:k * TILE + (s + 1) * P],
                                    wf16[:, bass.ds(e * WE + 2 * DC * HID + (wl * HC + k) * D, D)],
                                    start=(m == 0), stop=(m == 3 * HC - 1))
                                m += 1
                    last.then_inc(projected, 1)

            pipeline(pe, step)

        @block.vector
        def _(dve):
            v = nc.vector

            def take_x(t, u):
                wait(dve, x_hi_done, t + 1)
                v.tensor_tensor(xT[u][:, DC * TILE:2 * DC * TILE], ps_x[u][:, :], xT[u][:, 0:DC * TILE],
                                ALU.subtract).then_inc(x_lo_done, 1)

            take_x(0, 0)

            def step(j, u, now, after):
                t = 2 * j + u
                if now:
                    wait(dve, rows_in[u], 16 * (j + 1))
                    wait(dve, dest_f_done, t - 1)
                    v.tensor_copy(token[u][:, :], rows[u][:, :, META])
                    v.tensor_scalar(is_second[u][:, :], rows[u][:, :, META + 1], expert_f[:, bass.ds(t, 1)],
                                    float(TOKENS), ALU.is_equal, ALU.mult).then_inc(second_done, 1)
                if after:
                    take_x(t + 1, 1 - u)
                if now:
                    wait(dve, h_hi_done, t + 1)
                    wait(dve, projected, t - 1)
                    v.tensor_tensor(h_lo[u][:, :], h[u][:, :], h_hi[u][:, :], ALU.subtract).then_inc(h_lo_done, 1)
                if not (isinstance(t, int) and t == 0):
                    if isinstance(t, int) and t == 1:
                        dve.wait_ge(b2_in, 16)
                    e = dve.value_load(expert_i[0:1, bass.ds(t - 1, 1)], min_val=0, max_val=E - 1)
                    wait(dve, projected, t)
                    if not (isinstance(t, int) and t < 3):
                        wait(dve, scattered[1 - u], 32 * (j + u - 1))
                    v.scalar_tensor_tensor(out=y_out[1 - u][:, :].rearrange("p (s d) -> p s d", s=TS),
                                           in0=ps_y[1 - u][:, :].rearrange("p (s d) -> p s d", s=TS),
                                           scalar=1.0 / WSCALE,
                                           in1=b2[:, bass.ds(e * D, D)].unsqueeze(1).broadcast_to([P, TS, D]),
                                           op0=ALU.mult, op1=ALU.add).then_inc(y_ready, 1)

            pipeline(dve, step)

        @block.scalar
        def _(act):
            a = nc.scalar
            act.wait_ge(rows_in[1], 16)
            act.dma_start(b2[:, :], io["b2"].partition_broadcast(P)).then_inc(b2_in, 16)

            def take_x(t, u):
                wait(act, x_transposed, t + 1)
                wait(act, hidden, 2 * (t - 1))
                a.activation(xT[u][:, 0:DC * TILE], ps_x[u][:, :], ACT.Copy).then_inc(x_hi_done, 1)

            take_x(0, 0)

            def step(j, u, now, after):
                t = 2 * j + u
                if not now:
                    return
                e = act.value_load(expert_i[0:1, bass.ds(t, 1)], min_val=0, max_val=E - 1)
                wait(act, h_lo_done, t - 1)
                for c in range(HC):
                    if c % 2 == 0:
                        wait(act, hidden, 2 * t + c // 2 + 1)
                    last = a.activation(h[u][:, c * TILE:(c + 1) * TILE], ps_h[u][:, c * TILE:(c + 1) * TILE],
                                        ACT.Relu, scale=1.0 / WSCALE, bias=b1[:, bass.ds(e * HC + c, 1)])
                    if c % 2:
                        last.then_inc(relu_done, 1)
                if after:
                    take_x(t + 1, 1 - u)
                wait(act, relu_done, 2 * t + 2)
                wait(act, projected, t - 1)
                a.activation(h_hi[u][:, :], h[u][:, :], ACT.Copy).then_inc(h_hi_done, 1)

            pipeline(act, step)

        @block.gpsimd
        def _(pool):
            pool.wait_ge(b2_in, 16)
            b2_set = (b2_in, 16)

            def step(j, u, now, after):
                t = 2 * j + u
                if isinstance(t, int) and t == 0:
                    return
                wait(pool, second_done, t)
                if not (isinstance(t, int) and t < 3):
                    wait(pool, scattered[1 - u], 32 * (j + u - 1))
                nc.gpsimd.tensor_tensor(dest_f[:, :], is_second[1 - u][:, :], token[1 - u][:, :],
                                        ALU.add).then_inc(dest_f_done, 1)
                wait(pool, dest_f_done, t, beside=b2_set)
                nc.gpsimd.tensor_copy(dest[1 - u][:, :], dest_f[:, :]).then_inc(dest_done, 1)
                wait(pool, dest_done, t, beside=b2_set)
                wait(pool, y_ready, t, beside=b2_set)
                for s in range(TS):
                    nc.gpsimd.indirect_dma_start(outputs, bass.IndirectOffsetOnAxis(dest[1 - u][:, s:s + 1], 0),
                                                 y_out[1 - u][:, s * D:(s + 1) * D], None,
                                                 bounds_check=2 * TOKENS - 1,
                                                 oob_is_err=False).then_inc(scattered[1 - u], 16)

            pipeline(pool, step)
            pool.wait_ge(scattered[0], 32 * (TILES // 2 + 1))
            pool.wait_ge(scattered[1], 32 * (TILES // 2))


def build_combine(nc, io, keep):
    x1, cw = keep["x1"], keep["cw"]
    y2 = io["outputs"].rearrange("(k b s p) d -> k b p s d", k=2, b=NB, p=P)
    out = io["out"].rearrange("(b s p) d -> b p s d", b=NB, p=P)
    BUFS = 4
    with ExitStack() as ctx:
        def sb(name, shape, dt):
            return ctx.enter_context(nc.sbuf_tensor(name, shape, dt))

        def sem(name):
            return ctx.enter_context(nc.semaphore(name))

        first = [sb(f"first_{u}", [P, S, D], F32) for u in range(BUFS)]
        second = [sb(f"second_{u}", [P, S, D], F32) for u in range(BUFS)]
        both = [sb(f"both_{u}", [P, S, D], F32) for u in range(BUFS)]
        half_pow = sb("half_pow_2", [P, S], F32)
        eps = sb("eps_2", [P, S], F32)
        minus_one = sb("minus_one_2", [P, S], F32)
        bn = [sb(f"bn_2_{u}", [P, S, 6], F32) for u in range(2)]
        mv = [sb(f"mv_2_{u}", [P, S, 2], F32) for u in range(2)]
        rs = [sb(f"rs_2_{u}", [P, 3, S], F32) for u in range(2)]
        first_in = [sem(f"first_in_{u}") for u in range(BUFS)]
        second_in = [sem(f"second_in_{u}") for u in range(BUFS)]
        stored = [sem(f"stored_{u}") for u in range(BUFS)]
        set_done = sem("set_done_2")
        added = sem("added")
        weighted = sem("weighted")
        summed = sem("summed_2")
        bn_done = sem("bn_done_2")
        stats = sem("stats_2")
        rstd_step = sem("rstd_step_2")
        rstd = sem("rstd_2")
        norm_done = sem("norm_done")

        def pipeline(eng, step):
            for u in range(BUFS):
                step(0, u, True, u >= 1, u >= 2)
            with eng.Fori(1, NB // BUFS) as j:
                for u in range(BUFS):
                    step(j, u, True, True, True)
            step(NB // BUFS, 0, False, True, True)
            step(NB // BUFS, 1, False, False, True)

        block = ctx.enter_context(nc.Block())

        @block.sync
        def _(sp):
            def step(j, u, now, prev, prev2):
                if now:
                    wait(sp, added, BUFS * (j - 1) + u + 1)
                    sp.dma_start(first[u][:, :, :], y2[0, j * BUFS + u]).then_inc(first_in[u], 16)
                    wait(sp, summed, BUFS * (j - 1) + u + 1)
                    sp.dma_start(second[u][:, :, :], y2[1, j * BUFS + u]).then_inc(second_in[u], 16)

            pipeline(sp, step)

        @block.vector
        def _(dve):
            v = nc.vector
            v.memset(eps[:, :], LN_EPS / 4)
            v.memset(minus_one[:, :], -1.0)
            v.memset(half_pow[:, :], -0.5).then_inc(set_done, 1)

            def step(j, u, now, prev, prev2):
                i = BUFS * j + u
                w = u % 2
                if now:
                    wait(dve, rstd, i - 2)
                    wait(dve, first_in[u], 16 * (j + 1))
                    wait(dve, stored[u], 16 * j)
                    for s in range(S):
                        last = v.scalar_tensor_tensor(out=both[u][:, s, :], in0=first[u][:, s, :],
                                                      scalar=cw[:, bass.ds((i * S + s) * 2, 1)],
                                                      in1=x1[:, bass.ds((i * S + s) * D, D)],
                                                      op0=ALU.mult, op1=ALU.add)
                    last.then_inc(added, 1)
                if prev:
                    if not now:
                        wait(dve, rstd, i - 2)
                    wait(dve, bn_done, i, beside=(set_done, 1))
                    for s in range(S):
                        last = v.bn_aggr(mv[1 - w][:, s, :], bn[1 - w][:, s, :])
                    last.then_inc(stats, 1)
                if now:
                    wait(dve, added, i + 1)
                    wait(dve, weighted, i + 1)
                    v.tensor_tensor(both[u][:, :, :], both[u][:, :, :], second[u][:, :, :],
                                    ALU.add).then_inc(summed, 1)
                    wait(dve, summed, i + 1)
                    for s in range(S):
                        last = v.bn_stats(bn[w][:, s, :], both[u][:, s, :])
                    last.then_inc(bn_done, 1)

            pipeline(dve, step)

        @block.gpsimd
        def _(pool):
            g = nc.gpsimd
            pool.wait_ge(set_done, 1)

            def step(j, u, now, prev, prev2):
                i = BUFS * j + u
                if prev:
                    w = (u + 1) % 2
                    wait(pool, stats, i)
                    wait(pool, norm_done, i - 2)
                    g.tensor_tensor(rs[w][:, 2, :], mv[w][:, :, 0], minus_one[:, :], ALU.mult)
                    g.tensor_tensor(rs[w][:, 0, :], mv[w][:, :, 1], eps[:, :], ALU.add).then_inc(rstd_step, 1)
                    wait(pool, rstd_step, 2 * i - 1)
                    g.tensor_tensor(rs[w][:, 1, :], rs[w][:, 0, :], half_pow[:, :], ALU.pow).then_inc(rstd_step, 1)
                    wait(pool, rstd_step, 2 * i)
                    g.tensor_tensor(rs[w][:, 2, :], rs[w][:, 2, :], rs[w][:, 1, :], ALU.mult).then_inc(rstd, 1)

            pipeline(pool, step)

        @block.scalar
        def _(act):
            a = nc.scalar

            def step(j, u, now, prev, prev2):
                i = BUFS * j + u
                if now:
                    wait(act, second_in[u], 16 * (j + 1))
                    for s in range(S):
                        last = a.activation(second[u][:, s, :], second[u][:, s, :], ACT.Copy,
                                            scale=cw[:, bass.ds((i * S + s) * 2 + 1, 1)])
                    last.then_inc(weighted, 1)
                if prev2:
                    w, u2 = u % 2, (u + 2) % BUFS
                    wait(act, rstd, i - 1)
                    for s in range(S):
                        last = a.activation(both[u2][:, s, :], both[u2][:, s, :], ACT.Identity,
                                            scale=rs[w][:, 1, s:s + 1], bias=rs[w][:, 2, s:s + 1])
                    last.then_inc(norm_done, 1)
                    wait(act, norm_done, i - 1)
                    act.dma_start(out[i - 2], both[u2][:, :, :]).then_inc(stored[u2], 16)

            pipeline(act, step)
            for u in range(BUFS):
                act.wait_ge(stored[u], 16 * NB // BUFS)


def build(nc, io):
    io["region"] = nc.dram_tensor("region", [E * REGION + TILE, ROW], F32, kind="Internal").ap()
    io["outputs"] = nc.dram_tensor("outputs", [2 * TOKENS, D], F32, kind="Internal").ap()
    with ExitStack() as ctx:
        keep = {
            "x1": ctx.enter_context(nc.sbuf_tensor("x1", [P, NB * S * D], F32)),
            "wf16": ctx.enter_context(nc.sbuf_tensor("wf16", [P, E * 4 * DC * HID], F16)),
            "m8": ctx.enter_context(nc.sbuf_tensor("m8", [P, NB * S * E], F32)),
            "expert_f": ctx.enter_context(nc.sbuf_tensor("expert_f", [P, TILES], F32)),
            "expert_i": ctx.enter_context(nc.sbuf_tensor("expert_i", [P, TILES], I32)),
            "offset_i": ctx.enter_context(nc.sbuf_tensor("offset_i", [P, TILES], I32)),
            "ident": ctx.enter_context(nc.sbuf_tensor("ident", [P, P], F32)),
            "b1": ctx.enter_context(nc.sbuf_tensor("b1", [P, E * HC], F32)),
        }
        keep["cw"] = keep["m8"][:, 0:NB * S * 2]
        build_attend(nc, io, keep)
        build_experts(nc, io, keep)
        build_combine(nc, io, keep)


def kernel(**inputs):
    import numpy as np
    import concourse.bacc as bacc
    from concourse.bass_utils import run_bass_kernel_spmd

    x = inputs["L0_attn_x"].reshape(TOKENS, D)
    arrays = {
        "xT": x.reshape(NB, BLK, DC, P).transpose(0, 3, 2, 1).reshape(NB, P, DC * BLK),
        "x_tok": x.reshape(NB, S, P, D).transpose(0, 2, 1, 3),
        "wa": np.stack([inputs[f"L0_attn_{n}"].T.reshape(DC, P, D) for n in ("Wq", "Wv", "Wg", "Wo")], axis=2),
        "wf": np.stack([inputs["L0_ffn_W1"].reshape(E, DC, P, HID).transpose(0, 2, 1, 3).reshape(E, P, DC * HID),
                        inputs["L0_ffn_W2"].reshape(E, HC, P, D).transpose(0, 2, 1, 3).reshape(E, P, HC * D)],
                       axis=1).reshape(2 * E, P, DC * HID),
        "b1": inputs["L0_ffn_b1"].reshape(E * HC, P).T,
        "b2": inputs["L0_ffn_b2"].reshape(E * D),
        "gate_w": inputs["L0_ffn_gate_W"].reshape(DC, P, E).transpose(1, 0, 2),
        "ln_gb": np.stack([inputs["L0_attn_ln_g"].reshape(DC, P),
                           inputs["L0_attn_ln_b"].reshape(DC, P)]).transpose(2, 0, 1),
        "lam": np.repeat(inputs["L0_attn_decay"][:, 1, 0], D // 16).reshape(DC, P).T,
        "ident": np.eye(P, dtype=np.float32),
        "tri_ones": np.stack([np.triu(np.ones((P, P), np.float16), 1), np.ones((P, P), np.float16)], axis=1),
        "iota_e": np.tile(np.arange(E, dtype=np.float32), (P, 1)),
        "region_base": np.tile(np.arange(E, dtype=np.float32) * REGION, (P, 1)),
        "tile_iota": np.tile(np.arange(TILES, dtype=np.float32), (P, 1)),
        "token0": (np.arange(P)[:, None] + P * np.arange(S)[None, :]).astype(np.float32),
        "keep_state": np.tile((np.arange(NB + 1) % BLOCKS_PER_SEQ != 0).astype(np.float32), (P, 1)),
    }
    arrays = {n: np.ascontiguousarray(a) for n, a in arrays.items()}
    nc = bacc.Bacc("TRN2", target_bir_lowering=False, num_devices=1)
    io = {n: nc.dram_tensor(n + "_in", a.shape, mybir.dt.from_np(a.dtype), kind="ExternalInput").ap()
          for n, a in arrays.items()}
    io["out"] = nc.dram_tensor("out", [TOKENS, D], F32, kind="ExternalOutput").ap()
    build(nc, io)
    r = run_bass_kernel_spmd(nc, [{n + "_in": a for n, a in arrays.items()}], core_ids=[0])
    return r.results[0]["out"].reshape(inputs["L0_attn_x"].shape)
```
